# Optimizing a Trainium2 kernel written in Bass

```python
import numpy as np
import jax
import jax.numpy as jnp

def _softmax(x, axis=-1):
    return jax.nn.softmax(x, axis=axis)

def _gelu(x):
    return jax.nn.gelu(x, approximate=True)

def _silu(x):
    return jax.nn.silu(x)

def _sigmoid(x):
    return jax.nn.sigmoid(x)

def _layernorm(x, axis=-1, eps=1e-05):
    m = jnp.mean(x, axis=axis, keepdims=True)
    v = jnp.var(x, axis=axis, keepdims=True)
    return (x - m) / jnp.sqrt(v + eps)

def _scatter_add(tgt, idx, src, axis=0):
    return tgt.at[idx].add(src)

def _segment_sum(src, seg, n):
    return jax.ops.segment_sum(src, seg, n)
kernel_name = 'mk_cond_resid_d4_seqx_r4_186389'

def setup_inputs(seed: int=0):
    np.random.seed(seed)
    _w = jnp.asarray

    def _rec_inputs():
        import jax
        import jax.numpy as jnp
        _rk = jax.random.key(seed)
        x = -0.0002928 + 1 * jax.random.normal(jax.random.fold_in(_rk, 1), (8, 512, 256), jnp.float32)
        _lenS = 512 - jax.random.randint(jax.random.fold_in(_rk, 7), (8,), 0, max(1, 512 // 4) + 1, jnp.int32)
        _lenS2 = 512 - jax.random.randint(jax.random.fold_in(_rk, 8), (8,), 0, max(1, 512 // 4) + 1, jnp.int32)
        cond_1024 = 0.000887014 + 1.03683 * jax.random.normal(jax.random.fold_in(_rk, 11), (8, 256), jnp.float32)
        return (x, cond_1024)
    x, cond_1024 = _rec_inputs()

    def _L0_cond_setup():
        import jax, jax.numpy as jnp
        import numpy as np
        TOP_K = 2
        N_EXPERTS = 8
        N_SHARED = 1
        EPS = 1e-09
        key = jax.random.key(seed)
        ks = jax.random.split(key, 10)
        B, T, d = (2, 512, 256)
        h_s, h_r, E = (512, 128, N_EXPERTS)
        return {'x': jax.random.normal(ks[0], (B, T, d), jnp.float32), 't_emb': jax.random.normal(ks[1], (B, d), jnp.float32), 'router_w': jax.random.normal(ks[2], (E, d), jnp.float32) * 0.01, 'router_t_w': jax.random.normal(ks[3], (E, d), jnp.float32) * 0.01, 'router_bias': jnp.zeros((E,), jnp.float32), 'sw1': jax.random.normal(ks[4], (h_s, d), jnp.float32) * 0.02, 'sw3': jax.random.normal(ks[5], (h_s, d), jnp.float32) * 0.02, 'sw2': jax.random.normal(ks[6], (d, h_s), jnp.float32) * 0.02, 'rw1': jax.random.normal(ks[7], (E, h_r, d), jnp.float32) * 0.02, 'rw2': jax.random.normal(ks[8], (E, d, h_r), jnp.float32) * 0.02}
    _L0_cond_all = _L0_cond_setup()
    _L0_cond_in = {k: v for k, v in _L0_cond_all.items() if k in ('router_w', 'router_t_w', 'router_bias', 'sw1', 'sw3', 'sw2', 'rw1', 'rw2')}
    del _L0_cond_all

    def _L1_cond_setup():
        import jax, jax.numpy as jnp
        import numpy as np
        INV_SQRT2 = 0.7071067811865476
        key = jax.random.key(seed)
        k1, k2, k3, k4 = jax.random.split(key, 4)
        B, N, d = (8, 1024, 256)
        scale = 1.0 / np.sqrt(d)
        return {'v': jax.random.normal(k1, (B, N, d), dtype=jnp.float32), 'q_pool': jax.random.normal(k2, (B, d), dtype=jnp.float32), 'W1': jax.random.normal(k3, (d, d), dtype=jnp.float32) * scale, 'b1': jnp.zeros((d,), dtype=jnp.float32), 'W2': jax.random.normal(k4, (d, d), dtype=jnp.float32) * scale, 'b2': jnp.zeros((d,), dtype=jnp.float32)}
    _L1_cond_all = _L1_cond_setup()
    _L1_cond_in = {k: v for k, v in _L1_cond_all.items() if k in ('W1', 'b1', 'W2', 'b2')}
    del _L1_cond_all

    def _L2_cond_setup():
        import jax, jax.numpy as jnp
        import numpy as np
        RANK = 8
        LN_EPS = 1e-05
        key = jax.random.key(seed)
        ks = jax.random.split(key, 8)
        B, T, D = (16, 256, 256)
        A = 256
        I = 256
        OUT = D * RANK * 4
        s = 0.02
        return {'x': jax.random.normal(ks[0], (B, T, D), jnp.float32), 'ada_emb': jax.random.normal(ks[1], (B, A), jnp.float32), 'base_up': jax.random.normal(ks[2], (D, D), jnp.float32) * s, 'base_down': jax.random.normal(ks[3], (D, D), jnp.float32) * s, 'ln_gamma': jnp.ones((A,), jnp.float32), 'ln_beta': jnp.zeros((A,), jnp.float32), 'W1': jax.random.normal(ks[4], (A, I), jnp.float32) / np.sqrt(A), 'bias1': jnp.zeros((I,), jnp.float32), 'W2': jax.random.normal(ks[5], (I, OUT), jnp.float32) / np.sqrt(I), 'bias2': jnp.zeros((OUT,), jnp.float32)}
    _L2_cond_all = _L2_cond_setup()
    _L2_cond_in = {k: v for k, v in _L2_cond_all.items() if k in ('base_up', 'base_down', 'ln_gamma', 'ln_beta', 'W1', 'bias1', 'W2', 'bias2')}
    del _L2_cond_all

    def _L3_cond_setup():
        import jax, jax.numpy as jnp
        import numpy as np
        B, T, C = (64, 128, 256)
        key = jax.random.key(seed)
        ks = jax.random.split(key, 17)
        s_in = 1.0 / np.sqrt(C)

        def lin(kw, kb, fan_in):
            s = 1.0 / np.sqrt(fan_in)
            W = jax.random.uniform(kw, (C, fan_in), jnp.float32, -s, s)
            b = jax.random.uniform(kb, (C,), jnp.float32, -s, s)
            return (W, b)
        Wxz, bxz = lin(ks[0], ks[1], C)
        Whz, bhz = lin(ks[2], ks[3], C)
        Wxr, bxr = lin(ks[4], ks[5], C)
        Whr, bhr = lin(ks[6], ks[7], C)
        Wxh, bxh = lin(ks[8], ks[9], C)
        Whh, bhh = lin(ks[10], ks[11], C)
        Whq, bhq = lin(ks[12], ks[13], C)
        X = jax.random.normal(ks[14], (B, T, C), jnp.float32)
        h0 = jax.random.normal(ks[15], (B, C), jnp.float32)
        return {'X': X, 'h0': h0, 'Wxz': Wxz, 'bxz': bxz, 'Whz': Whz, 'bhz': bhz, 'Wxr': Wxr, 'bxr': bxr, 'Whr': Whr, 'bhr': bhr, 'Wxh': Wxh, 'bxh': bxh, 'Whh': Whh, 'bhh': bhh, 'Whq': Whq, 'bhq': bhq}
    _L3_cond_all = _L3_cond_setup()
    _L3_cond_in = {k: v for k, v in _L3_cond_all.items() if k in ('Wxz', 'bxz', 'Whz', 'bhz', 'Wxr', 'bxr', 'Whr', 'bhr', 'Wxh', 'bxh', 'Whh', 'bhh', 'Whq', 'bhq')}
    del _L3_cond_all
    return {'x': x, 'cond_1024': cond_1024, 'L0_cond_router_w': _L0_cond_in['router_w'], 'L0_cond_router_t_w': _L0_cond_in['router_t_w'], 'L0_cond_router_bias': _L0_cond_in['router_bias'], 'L0_cond_sw1': _L0_cond_in['sw1'], 'L0_cond_sw3': _L0_cond_in['sw3'], 'L0_cond_sw2': _L0_cond_in['sw2'], 'L0_cond_rw1': _L0_cond_in['rw1'], 'L0_cond_rw2': _L0_cond_in['rw2'], 'L1_cond_W1': _L1_cond_in['W1'], 'L1_cond_b1': _L1_cond_in['b1'], 'L1_cond_W2': _L1_cond_in['W2'], 'L1_cond_b2': _L1_cond_in['b2'], 'L2_cond_base_up': _L2_cond_in['base_up'], 'L2_cond_base_down': _L2_cond_in['base_down'], 'L2_cond_ln_gamma': _L2_cond_in['ln_gamma'], 'L2_cond_ln_beta': _L2_cond_in['ln_beta'], 'L2_cond_W1': _L2_cond_in['W1'], 'L2_cond_bias1': _L2_cond_in['bias1'], 'L2_cond_W2': _L2_cond_in['W2'], 'L2_cond_bias2': _L2_cond_in['bias2'], 'L3_cond_Wxz': _L3_cond_in['Wxz'], 'L3_cond_bxz': _L3_cond_in['bxz'], 'L3_cond_Whz': _L3_cond_in['Whz'], 'L3_cond_bhz': _L3_cond_in['bhz'], 'L3_cond_Wxr': _L3_cond_in['Wxr'], 'L3_cond_bxr': _L3_cond_in['bxr'], 'L3_cond_Whr': _L3_cond_in['Whr'], 'L3_cond_bhr': _L3_cond_in['bhr'], 'L3_cond_Wxh': _L3_cond_in['Wxh'], 'L3_cond_bxh': _L3_cond_in['bxh'], 'L3_cond_Whh': _L3_cond_in['Whh'], 'L3_cond_bhh': _L3_cond_in['bhh'], 'L3_cond_Whq': _L3_cond_in['Whq'], 'L3_cond_bhq': _L3_cond_in['bhq']}

def reference(x, cond_1024, L0_cond_router_w, L0_cond_router_t_w, L0_cond_router_bias, L0_cond_sw1, L0_cond_sw3, L0_cond_sw2, L0_cond_rw1, L0_cond_rw2, L1_cond_W1, L1_cond_b1, L1_cond_W2, L1_cond_b2, L2_cond_base_up, L2_cond_base_down, L2_cond_ln_gamma, L2_cond_ln_beta, L2_cond_W1, L2_cond_bias1, L2_cond_W2, L2_cond_bias2, L3_cond_Wxz, L3_cond_bxz, L3_cond_Whz, L3_cond_bhz, L3_cond_Wxr, L3_cond_bxr, L3_cond_Whr, L3_cond_bhr, L3_cond_Wxh, L3_cond_bxh, L3_cond_Whh, L3_cond_bhh, L3_cond_Whq, L3_cond_bhq):
    import jax
    import jax.numpy as jnp

    def _L0_cond_ref(x, t_emb, router_w, router_t_w, router_bias, sw1, sw3, sw2, rw1, rw2):
        import jax, jax.numpy as jnp
        import numpy as np
        TOP_K = 2
        N_EXPERTS = 8
        N_SHARED = 1
        EPS = 1e-09
        B, T, C = x.shape
        N = B * T
        x_flat = x.reshape(N, C)
        shared_out = jnp.einsum('nh,dh->nd', jax.nn.silu(x_flat @ sw1.T) * (x_flat @ sw3.T), sw2)
        t_bias = t_emb @ router_t_w.T
        t_bias_flat = jnp.broadcast_to(t_bias[:, None, :], (B, T, N_EXPERTS)).reshape(N, N_EXPERTS)
        s = jax.nn.sigmoid((x_flat @ router_w.T + t_bias_flat).astype(jnp.float32))
        sel_scores = s + router_bias
        _, topk_idx = jax.lax.top_k(sel_scores, TOP_K)
        s_sel = jnp.take_along_axis(s, topk_idx, axis=1)
        denom = jnp.sum(s_sel, axis=1, keepdims=True)
        gates = jnp.where(denom > EPS, s_sel / (denom + EPS), 1.0 / TOP_K).astype(x.dtype)
        combine = jnp.sum(gates[:, :, None] * jax.nn.one_hot(topk_idx, N_EXPERTS, dtype=x.dtype), axis=1)
        H = jax.nn.gelu(jnp.einsum('nd,ehd->enh', x_flat, rw1), approximate=False)
        O = jnp.einsum('enh,edh->end', H, rw2)
        routed_out = jnp.einsum('end,ne->nd', O, combine)
        out = (shared_out + routed_out) / (N_SHARED + TOP_K)
        return out.reshape(B, T, C)

    def _L1_cond_ref(v, q_pool, W1, b1, W2, b2):
        import jax, jax.numpy as jnp
        import numpy as np
        INV_SQRT2 = 0.7071067811865476
        B, N, d = v.shape
        h = jax.nn.silu(q_pool @ W1.T + b1)
        gate = jax.nn.sigmoid(h @ W2.T + b2)[:, None, :]
        levels = int(np.log2(N))
        a = v
        details = []
        for _ in range(levels):
            e, o = (a[:, 0::2], a[:, 1::2])
            details.append((e - o) * INV_SQRT2)
            a = (e + o) * INV_SQRT2
        a = a * gate
        for dc in reversed(details):
            dc = dc * gate
            e = (a + dc) * INV_SQRT2
            o = (a - dc) * INV_SQRT2
            n = e.shape[1]
            a = jnp.stack([e, o], axis=2).reshape(B, 2 * n, d)
        return v + a

    def _L2_cond_ref(x, ada_emb, base_up, base_down, ln_gamma, ln_beta, W1, bias1, W2, bias2):
        import jax, jax.numpy as jnp
        import numpy as np
        RANK = 8
        LN_EPS = 1e-05
        B, T, D = x.shape
        R = RANK
        mu = jnp.mean(ada_emb, axis=-1, keepdims=True)
        var = jnp.mean(jnp.square(ada_emb - mu), axis=-1, keepdims=True)
        c = (ada_emb - mu) / jnp.sqrt(var + LN_EPS) * ln_gamma + ln_beta
        h = jax.nn.gelu(c @ W1 + bias1, approximate=False)
        w = h @ W2 + bias2
        a1, b1, a2, b2 = [t.reshape(B, D, R) for t in jnp.split(w, 4, axis=-1)]
        u = jnp.einsum('btd,bdr->btr', x, a2)
        mid = jnp.einsum('btd,dl->btl', x, base_down) + jnp.einsum('btr,blr->btl', u, b2)
        mid = jax.nn.gelu(mid, approximate=False)
        v = jnp.einsum('blr,btl->btr', b1, mid)
        out = jnp.einsum('btl,kl->btk', mid, base_up) + jnp.einsum('bkr,btr->btk', a1, v)
        return x + out

    def _L3_cond_ref(X, h0, Wxz, bxz, Whz, bhz, Wxr, bxr, Whr, bhr, Wxh, bxh, Whh, bhh, Whq, bhq):
        import jax, jax.numpy as jnp
        import numpy as np
        B, T, C = (64, 128, 256)
        Xz = jnp.einsum('btc,hc->tbh', X, Wxz) + bxz
        Xr = jnp.einsum('btc,hc->tbh', X, Wxr) + bxr
        Xh = jnp.einsum('btc,hc->tbh', X, Wxh) + bxh

        def step(H, xs):
            xz, xr, xh = xs
            Z = jax.nn.sigmoid(xz + H @ Whz.T + bhz)
            R = jax.nn.sigmoid(xr + H @ Whr.T + bhr)
            H_tilda = jnp.tanh(xh + R * H @ Whh.T + bhh)
            H_new = Z * H + (1.0 - Z) * H_tilda
            Y = H_new @ Whq.T + bhq
            return (H_new, Y)
        _, Ys = jax.lax.scan(step, h0, (Xz, Xr, Xh))
        return jnp.transpose(Ys, (1, 0, 2))
    x = x + _L0_cond_ref(x, cond_1024, L0_cond_router_w, L0_cond_router_t_w, L0_cond_router_bias, L0_cond_sw1, L0_cond_sw3, L0_cond_sw2, L0_cond_rw1, L0_cond_rw2)
    x = x + _L1_cond_ref(x, cond_1024, L1_cond_W1, L1_cond_b1, L1_cond_W2, L1_cond_b2)
    x = x + _L2_cond_ref(x, cond_1024, L2_cond_base_up, L2_cond_base_down, L2_cond_ln_gamma, L2_cond_ln_beta, L2_cond_W1, L2_cond_bias1, L2_cond_W2, L2_cond_bias2)
    x = x + _L3_cond_ref(x, cond_1024, L3_cond_Wxz, L3_cond_bxz, L3_cond_Whz, L3_cond_bhz, L3_cond_Wxr, L3_cond_bxr, L3_cond_Whr, L3_cond_bhr, L3_cond_Wxh, L3_cond_bxh, L3_cond_Whh, L3_cond_bhh, L3_cond_Whq, L3_cond_bhq)
    return x

_drawn_inputs = setup_inputs


def setup_inputs(seed=0):
    import zlib

    import numpy as np

    out = dict(_drawn_inputs(seed))
    spreads = {'L0_cond_router_bias': (0.0, 0.768),
     'L1_cond_b1': (0.0, 0.8),
     'L1_cond_b2': (0.0, 0.8),
     'L2_cond_ln_gamma': (1.0, 0.2),
     'L2_cond_ln_beta': (0.0, 0.1),
     'L2_cond_bias1': (0.0, 0.1),
     'L2_cond_bias2': (0.0, 0.1)}
    factors = {'L0_cond_router_w': 8.0,
     'L0_cond_router_t_w': 8.0,
     'L0_cond_sw1': 7.049,
     'L0_cond_sw3': 6.947,
     'L0_cond_sw2': 6.848,
     'L0_cond_rw1': 6.133,
     'L0_cond_rw2': 6.005,
     'L2_cond_base_up': 3.933,
     'L2_cond_base_down': 3.835,
     'L3_cond_Wxz': 200.0,
     'L3_cond_bxz': 200.0,
     'L3_cond_Whz': 200.0,
     'L3_cond_bhz': 200.0,
     'L3_cond_Wxr': 200.0,
     'L3_cond_bxr': 64.0,
     'L3_cond_Whr': 64.0,
     'L3_cond_bhr': 64.0,
     'L3_cond_Wxh': 200.0,
     'L3_cond_bxh': 200.0,
     'L3_cond_Whh': 200.0,
     'L3_cond_bhh': 200.0,
     'L3_cond_Whq': 200.0,
     'L3_cond_bhq': 200.0}
    for name, (base, spread) in spreads.items():
        noise = np.random.default_rng([zlib.crc32(name.encode()), seed]).standard_normal(out[name].shape)
        drawn = base * np.exp(spread * noise) if base else spread * noise
        out[name] = jnp.asarray(drawn.astype(out[name].dtype))
    for name, factor in factors.items():
        out[name] = (out[name] * factor).astype(out[name].dtype)
    return out
```

```python
from contextlib import ExitStack

import numpy as np
import concourse.bass as bass
from concourse import mybir

ALU = mybir.AluOpType
ACT = mybir.ActivationFunctionType
F32 = mybir.dt.float32
BF16 = mybir.dt.bfloat16
U32 = mybir.dt.uint32
AX_X = mybir.AxisListType.X

P = 128
B, T, D = 8, 512, 256
KC = D // P
TOK = P
STEPS = TOK // B
BLOCKS = T // STEPS
HS = 512
EXPERTS, HR = 8, 128
RANK = 8
BR = B * RANK
ADAPT = 4 * RANK * D
PARTS = 3
GATE_OPS = 13
Z, R, H = range(3)
EPS_GATE, EPS_LN = 1e-9, 1e-5


def count(m, per, extra=0):
    return m[0] * (2 * per) + ((m[1] + 1) * per + extra)


def pair_count(m, per):
    return m[0] * per + (m[1] // 2 + 1) * per


def step_count(m, s):
    return m[0] * (2 * STEPS) + (m[1] * STEPS + s + 1)


def token_start(m):
    return m[0] * (2 * TOK) + m[1] * TOK


def build(nc, a, out):
    with ExitStack() as ctx:
        def sb(name, shape, dt=F32):
            return ctx.enter_context(nc.sbuf_tensor(name, shape, dt))

        def ps(name, shape=(P, 512), dt=F32):
            return ctx.enter_context(nc.psum_tensor(name, list(shape), dt))

        def sem(name):
            return ctx.enter_context(nc.semaphore(name))

        sw1 = sb("sw1", [P, KC, HS])
        sw3 = sb("sw3", [P, KC, HS])
        sw2 = sb("sw2", [P, HS // P, D])
        rw1 = sb("rw1", [P, KC, EXPERTS * HR])
        rw2 = sb("rw2", [P, EXPERTS, D])
        rw = sb("rw", [P, KC, EXPERTS])
        rtw = sb("rtw", [P, KC, EXPERTS])
        rbias = sb("rbias", [P, EXPERTS])
        l1w1 = sb("l1w1", [P, KC, D])
        l1w2 = sb("l1w2", [P, KC, D])
        l1b = sb("l1b", [P, 2, KC])
        down = sb("down", [P, KC, D])
        up = sb("up", [P, KC, D])
        aw1 = sb("aw1", [P, KC, D])
        aw2 = sb("aw2", [P, KC, ADAPT])
        lnab = sb("lnab", [P, 3, KC])
        abias = sb("abias", [BR, 4, D])
        wx = sb("wx", [P, 3, KC, D])
        wh = sb("wh", [P, 3, KC, D])
        wrest = sb("wrest", [P, 3, KC, D])
        whp = sb("whp", [P, PARTS, 3, KC, D], BF16)
        wq = sb("wq", [P, KC, D])
        wqh = sb("wqh", [P, KC, D])
        bx = sb("bx", [P, 3, KC])
        bh = sb("bh", [P, 3, KC])
        bxh = sb("bxh", [P, 3, KC])
        bq = sb("bq", [P, KC])
        ident = sb("ident", [P, P])
        identb = sb("identb", [P, P], BF16)
        iota = sb("iota", [P, EXPERTS])
        own = sb("own", [BR, TOK])
        cond_tok = sb("cond_tok", [P, KC, TOK])
        condT = cond_tok[:, :, 0:B]
        cond = sb("cond", [B, D])

        tbias = sb("tbias", [P, EXPERTS])
        l1pre = sb("l1pre", [P, KC, B])
        l1sig = sb("l1sig", [P, KC, B])
        l1h = sb("l1h", [P, KC, B])
        gate2 = sb("gate2", [P, KC, B])
        stats = sb("stats", [B, 6])
        meanvar = sb("meanvar", [B, 2])
        lnv = sb("lnv", [B, 3])
        cn = sb("cn", [B, D])
        cT = sb("cT", [P, KC, B])
        ah = sb("ah", [P, KC, B])
        wrow = sb("wrow", [B, ADAPT])
        low = sb("low", [BR, 4, D])
        a2b1 = sb("a2b1", [P, 2, KC, BR])

        xt = sb("xt", [P, 2, KC, TOK])
        holder = sb("holder", [P, 1])
        score = sb("score", [P, EXPERTS])
        euler = sb("euler", [P, EXPERTS])
        expn = sb("expn", [P, EXPERTS])
        exp1 = sb("exp1", [P, EXPERTS])
        sg = sb("sg", [P, EXPERTS])
        sel = sb("sel", [P, EXPERTS])
        top8 = sb("top8", [P, 8])
        idx = sb("idx", [P, 8], U32)
        idxf = sb("idxf", [P, 2])
        first = sb("first", [P, EXPERTS])
        chosen = sb("chosen", [P, EXPERTS])
        ssel = sb("ssel", [P, EXPERTS])
        den = sb("den", [P, 4])
        scaled = sb("scaled", [P, EXPERTS])
        comb = sb("comb", [P, EXPERTS])
        sig1 = sb("sig1", [P, HS])
        sa = sb("sa", [P, HS])
        gs = sb("gs", [P, HS])
        pe_e = sb("pe_e", [P, 2, 4 * TOK])
        ge = sb("ge", [P, 2, 4 * TOK])
        x1 = sb("x1", [P, KC, TOK])
        x2 = sb("x2", [P, KC, TOK])
        g2 = sb("g2", [P, KC, TOK])
        um = sb("um", [BR, TOK])
        vm = sb("vm", [BR, TOK])
        x3 = sb("x3", [P, 2, KC, TOK])
        xp = aw2[:, 0, 0:2 * PARTS * 3 * KC * TOK].rearrange("p (u a g k t) -> p u a g k t", u=2, a=PARTS, g=3, k=KC)
        hist = aw2[:, 1, 0:2 * PARTS * KC * TOK].rearrange("p (u a k t) -> p u a k t", u=2, a=PARTS, k=KC)
        rh = sb("rh", [P, PARTS, KC, B])
        rg = sb("rg", [P, KC, B])
        zg = sb("zg", [P, KC, B])
        zsum = sb("zsum", [P, KC, B])
        zh = sb("zh", [P, KC, B])
        ht = sb("ht", [P, KC, B])
        fresh = sb("fresh", [P, KC, B])
        osb = sb("osb", [P, KC, TOK])

        xpv = xp.bitcast(BF16)
        histv = hist.bitcast(BF16)
        rhv = rh[:].bitcast(BF16)

        def xp_part(par, part, g, s):
            return xpv[:, par, part, g, :, 2 * s * B + 1:2 * (s + 1) * B:2]

        def xp_all(par, g, s):
            return xpv[:, par, :, g, :, 2 * s * B + 1:2 * (s + 1) * B:2].rearrange("p a k c -> p k a c")

        def hist_part(par, part, k, s):
            return histv[:, par, part, k, 2 * s * B + 1:2 * (s + 1) * B:2]

        def hist_all(par, k, s):
            return histv[:, par, :, k, 2 * s * B + 1:2 * (s + 1) * B:2]

        def before(par, s):
            return (par, s - 1) if s else (1 - par, STEPS - 1)

        p_r, p_z, p_h = ps("p_r"), ps("p_z"), ps("p_h")
        bank = [ps(f"bank{i}") for i in range(5)]
        A1, A3, E47, D4, E5 = bank
        pr = p_r[:, 0:KC * B].rearrange("p (k c) -> p k c", k=KC)
        ph = p_h[:, 0:KC * B].rearrange("p (k c) -> p k c", k=KC)
        pz = p_z[:, 0:KC * PARTS * B].rearrange("p (k a c) -> p k a c", k=KC, a=PARTS)
        y_ps = D4[:, 0:KC * TOK].rearrange("p (k t) -> p k t", k=KC)
        score_ps = D4[:, 0:EXPERTS]
        l0_ps = E5[:, 0:KC * TOK].rearrange("p (k t) -> p k t", k=KC)
        mid_ps = E5[:, 0:KC * TOK].rearrange("p (k t) -> p k t", k=KC)
        low_ps = E5[0:BR, KC * TOK:(KC + 1) * TOK]
        proj_ps = E5[:, :].rearrange("p (g k t) -> p g k t", g=2, k=KC)

        cond_in, l1_in, ad_in, ad2_in, l0_in, l0r_in, l2_in, rec_in, const_in, wx_in = (
            sem(n) for n in ("cond_in", "l1_in", "ad_in", "ad2_in", "l0_in", "l0r_in", "l2_in", "rec_in",
                             "const_in", "wx_in"))
        abias_in, bias_in, wq_in, setup_pool = (sem(n) for n in ("abias_in", "bias_in", "wq_in", "setup_pool"))
        x_in = [sem("x_in0"), sem("x_in1")]
        stored = sem("stored")
        low_in = sem("low_in")
        split_w, setup_pe, setup_act, setup_dve, wrow_dve, adapt_pe, lowT_pe, ready_dve = (
            sem(n) for n in ("split_w", "setup_pe", "setup_act", "setup_dve", "wrow_dve", "adapt_pe", "lowT_pe",
                             "ready_dve"))
        names = ("scores_done", "a1_done", "a3_done", "ex47_done", "ex03_done", "cb47_done", "cb03_done", "l0_done",
                 "u_done", "mid_done", "v_done", "l2_done", "projrz_done", "projh_done", "y_done",
                 "score_exp", "a1_sig", "xprz_done", "xph_done",
                 "score_in", "gating", "sa_done", "gs_done", "pe47_done", "ge47_done", "pe03_done", "ge03_done",
                 "x1_done", "x2_done", "um_done", "g2_done", "vm_done", "x3_done", "rz_mid", "rz_low", "h_mid_x",
                 "h_low_x", "out_done")
        (scores_done, a1_done, a3_done, ex47_done, ex03_done, cb47_done, cb03_done, l0_done,
         u_done, mid_done, v_done, l2_done, projrz_done, projh_done, y_done,
         score_exp, a1_sig, xprz_done, xph_done,
         score_in, gating, sa_done, gs_done, pe47_done, ge47_done, pe03_done, ge03_done,
         x1_done, x2_done, um_done, g2_done, vm_done, x3_done, rz_mid, rz_low, h_mid_x,
         h_low_x, out_done) = (sem(n) for n in names)
        (r_done, z_done, h_done, rg_done, zg_done, ht_done, rh_hi, rh_mid, rh_low, zsum_done, zh_done,
         fresh_done, st_hi, st_mid, st_low) = (
            sem(n) for n in ("r_done", "z_done", "h_done", "rg_done", "zg_done", "ht_done", "rh_hi",
                             "rh_mid", "rh_low", "zsum_done", "zh_done", "fresh_done", "st_hi", "st_mid", "st_low"))

        block = ctx.enter_context(nc.Block())

        def blocks(eng, body):
            body((0, 0), 0, False, True, True)
            with eng.Fori(0, (BLOCKS - 4) // 2) as j:
                body((j, 1), 1, True, True, True)
                body((j, 2), 0, True, True, True)
            body((0, BLOCKS - 3), 1, True, True, True)
            body((0, BLOCKS - 2), 0, True, True, False)
            body((0, BLOCKS - 1), 1, True, False, False)

        def later(m, d):
            return (m[0], m[1] + d)

        @block.sync
        def _(sp):
            sp.dma_start(cond_tok[:], a["cond_tok"]).then_inc(cond_in, 16)
            sp.dma_start(cond[:], a["cond"]).then_inc(cond_in, 16)
            sp.dma_start(rw[:], a["rw"]).then_inc(l0_in, 16)
            sp.dma_start(rtw[:], a["rtw"]).then_inc(l0_in, 16)
            sp.dma_start(sw1[:], a["sw1"]).then_inc(l0_in, 16)
            sp.dma_start(aw1[:], a["aw1"]).then_inc(ad_in, 16)
            sp.dma_start(lnab[:], a["lnab"]).then_inc(ad_in, 16)
            sp.dma_start(sw3[:], a["sw3"]).then_inc(l0_in, 16)
            sp.dma_start(rw1[:], a["rw1"]).then_inc(l0r_in, 16)
            sp.dma_start(sw2[:], a["sw2"]).then_inc(l0r_in, 16)
            sp.dma_start(rw2[:], a["rw2"]).then_inc(l0r_in, 16)
            for k in range(KC):
                sp.dma_start(aw2[:, k], a["aw2"][:, k], max_dma_last_dim=8192).then_inc(ad2_in, 16)
            sp.dma_start(down[:], a["down"]).then_inc(l2_in, 16)
            sp.dma_start(up[:], a["up"]).then_inc(l2_in, 16)
            for g in range(3):
                sp.dma_start(wx[:, g], a["wx"][g]).then_inc(wx_in, 16)
            sp.dma_start(wq[:], a["wq"]).then_inc(wq_in, 16)
            for i in range(4):
                sp.wait_ge(wrow_dve, 4 * (i + 1))
                for b in range(B):
                    src = wrow[b:b + 1, i * RANK * D:(i + 1) * RANK * D].rearrange("b (r d) -> b r d", r=RANK)
                    sp.dma_start(low[b * RANK:(b + 1) * RANK, i, :], src).then_inc(low_in, 16)

        @block.gpsimd
        def _(pool):
            pool.dma_start(xt[:, 0], a["xT"][:, :, 0:TOK]).then_inc(x_in[0], 16)
            pool.dma_start(ident[:], a["ident"]).then_inc(const_in, 16)
            pool.dma_start(iota[:], a["iota"]).then_inc(const_in, 16)
            pool.dma_start(own[:], a["own"]).then_inc(const_in, 16)
            pool.dma_start(rbias[:], a["rbias"].partition_broadcast(P)).then_inc(const_in, 16)
            pool.dma_start(xt[:, 1], a["xT"][:, :, TOK:2 * TOK]).then_inc(x_in[1], 16)
            for g in range(3):
                pool.dma_start(wh[:, g], a["wh"][g]).then_inc(rec_in, 16)
            pool.dma_start(l1w1[:], a["l1w1"]).then_inc(l1_in, 16)
            pool.dma_start(l1w2[:], a["l1w2"]).then_inc(l1_in, 16)
            pool.dma_start(l1b[:], a["l1b"]).then_inc(l1_in, 16)
            pool.dma_start(bx[:], a["bx"]).then_inc(bias_in, 16)
            pool.dma_start(bh[:], a["bh"]).then_inc(bias_in, 16)
            pool.dma_start(bq[:], a["bq"]).then_inc(bias_in, 16)
            for b in range(B):
                pool.dma_start(abias[b * RANK:(b + 1) * RANK], a["abias"]).then_inc(abias_in, 16)
            pool.wait_ge(setup_dve, 3)
            pool.tensor_tensor(lnv[:, 2:3], lnv[:, 0:1], lnv[:, 1:2], ALU.pow).then_inc(setup_pool, 1)
            pool.wait_ge(rec_in, 48)
            for g, scale in ((Z, 0.5), (R, 0.5), (H, 0.25)):
                pool.tensor_scalar(wrest[:, g], wh[:, g], scale, None, ALU.mult).then_inc(split_w, 1)
            pool.wait_ge(split_w, 3)
            pool.tensor_copy(whp[:, 0], wrest[:]).then_inc(split_w, 1)
            pool.wait_ge(split_w, 4)
            pool.tensor_tensor(wh[:], wrest[:], whp[:, 0], ALU.subtract).then_inc(split_w, 1)
            pool.wait_ge(split_w, 5)
            pool.tensor_copy(whp[:, 1], wh[:]).then_inc(split_w, 1)
            pool.wait_ge(split_w, 6)
            pool.tensor_tensor(wrest[:], wh[:], whp[:, 1], ALU.subtract).then_inc(split_w, 1)
            pool.wait_ge(split_w, 7)
            pool.tensor_copy(whp[:, 2], wrest[:]).then_inc(split_w, 1)
            pool.wait_ge(wq_in, 16)
            pool.tensor_scalar(wqh[:], wq[:], 0.5, None, ALU.mult).then_inc(split_w, 1)

            def exp_scores(m):
                pool.wait_ge(score_in, count(m, 1))
                pool.tensor_tensor(expn[:], euler[:], score[:], ALU.pow).then_inc(score_exp, 1)

            pool.memset(euler[:], float(np.e)).then_inc(setup_pool, 1)
            pool.wait_ge(setup_pool, 2)
            exp_scores((0, 0))

            def xcols(m):
                at = token_start(m)
                return at if type(at) is int else pool.snap(at)

            def load_x(at, par):
                pool.dma_start(xt[:, par], a["xT"][:, :, bass.ds(at, TOK)]).then_inc(x_in[par], 16)

            def store(m):
                at = xcols(m)
                pool.wait_ge(out_done, count(m, 1))
                pool.dma_start(out[:, :, bass.ds(at, TOK)], osb[:]).then_inc(stored, 16)

            pool.wait_ge(x1_done, 1)
            load_x(2 * TOK, 0)
            exp_scores((0, 1))

            def body(m, par, has_y, has_l23, has_l0):
                if has_l0 and not (type(m[0]) is int and m[1] + 3 >= BLOCKS):
                    x_block = xcols(later(m, 3))
                    pool.wait_ge(x1_done, count(later(m, 1), 1))
                    load_x(x_block, 1 - par)
                if has_y:
                    store(later(m, -1))
                if has_l0:
                    exp_scores(later(m, 2))

            blocks(pool, body)
            store((0, BLOCKS - 1))
            pool.wait_ge(stored, 16 * BLOCKS)


        @block.tensor
        def _(pe):
            def mm(o, w, x, start, stop):
                return pe.matmul(o, w, x, start=start, stop=stop, skip_group_check=True)

            def scores(m, par):
                pe.wait_ge(x_in[par], pair_count(m, 16))
                for k in range(KC):
                    i = mm(score_ps, xt[:, par, k], rw[:, k], k == 0, k == KC - 1)
                i.then_inc(scores_done, 1)

            def up_chunks(ps_, w, par, chunks, done, last):
                for c in chunks:
                    for k in range(KC):
                        i = mm(ps_[:, c % 4 * TOK:(c % 4 + 1) * TOK], w[:, k, c * P:(c + 1) * P], xt[:, par, k],
                               k == 0, k == KC - 1)
                if last:
                    i.then_inc(done, 1)

            def spread_gates(m, ps_, experts, done, last):
                pe.wait_ge(gating, count(m, GATE_OPS))
                for e in experts:
                    i = mm(ps_[:, e % 4 * TOK:(e % 4 + 1) * TOK], comb[:, e:e + 1].to_broadcast([P, P]), ident[:],
                           True, True)
                if last:
                    i.then_inc(done, 1)

            def l0_out(half, kind, chunks, start=False, done=None):
                for c in chunks:
                    w = sw2 if kind == "s" else rw2
                    g = gs[:, c * TOK:(c + 1) * TOK] if kind == "s" else ge[:, c // 4, c % 4 * TOK:(c % 4 + 1) * TOK]
                    i = mm(l0_ps[:, half], w[:, c, half * P:(half + 1) * P], g, start and c == chunks[0], False)
                if done is not None:
                    i.then_inc(done, 1)

            def mid_base(m):
                pe.wait_ge(x2_done, count(m, 1))
                for half in range(KC):
                    for k in range(KC):
                        mm(mid_ps[:, half], down[:, k, half * P:(half + 1) * P], x2[:, k],
                           half == 0 and k == 0, False)
                for k in range(KC):
                    i = mm(low_ps, a2b1[:, 0, k], x2[:, k], False, k == KC - 1)
                i.then_inc(u_done, 1)

            def mid_low(m):
                pe.wait_ge(um_done, count(m, 1))
                for half in range(KC):
                    i = mm(mid_ps[:, half], low[:, 3, half * P:(half + 1) * P], um[:], False, True)
                i.then_inc(mid_done, 1)

            def up_base(m):
                pe.wait_ge(g2_done, count(m, 1))
                for half in range(KC):
                    for k in range(KC):
                        mm(mid_ps[:, half], up[:, k, half * P:(half + 1) * P], g2[:, k], half == 0 and k == 0, False)
                for k in range(KC):
                    i = mm(low_ps, a2b1[:, 1, k], g2[:, k], False, k == KC - 1)
                i.then_inc(v_done, 1)

            def up_low(m):
                pe.wait_ge(vm_done, count(m, 1))
                for half in range(KC):
                    i = mm(mid_ps[:, half], low[:, 0, half * P:(half + 1) * P], vm[:], False, True)
                i.then_inc(l2_done, 1)

            def project(par, slot, g, half, done=None):
                for k in range(KC):
                    i = mm(proj_ps[:, slot, half], wx[:, g, k, half * P:(half + 1) * P], x3[:, par, k],
                           k == 0, k == KC - 1)
                if done is not None:
                    i.then_inc(done, 1)

            def y_out(m, par, waited):
                pe.wait_ge(st_hi, step_count(m, STEPS - 1) + 1)
                for half in range(KC):
                    for k in range(KC):
                        i = mm(y_ps[:, half], wqh[:, k, half * P:(half + 1) * P], hist[:, par, 0, k], k == 0, k == KC - 1)
                i.then_inc(y_done, 1)

            def inject(p_, par, g, s):
                for part in range(PARTS):
                    mm(p_, identb[:], xp_part(par, part, g, s), part == 0, False)

            def recur(p_, g, parts, done):
                for part, (ready, at, view) in enumerate(parts):
                    pe.wait_ge(ready, at)
                    for wpart in range(PARTS - part):
                        for half in range(KC):
                            for k in range(KC):
                                i = mm(p_[:, half], whp[:, wpart, g, k, half * P:(half + 1) * P], view(k), False,
                                       part == PARTS - 1)
                i.then_inc(done, 1)

            def step(m, par, s, first_in_block):
                n = step_count(m, s)
                bp, bs = before(par, s)
                if first_in_block:
                    pe.wait_ge(h_low_x, count(m, 1))
                    pe.wait_ge(rz_low, count(m, 1))
                    inject(pr, par, R, s)
                recur(pr, R, [(q, n, lambda k, part=part: hist_part(bp, part, k, bs))
                              for part, q in enumerate((st_hi, st_mid, st_low))], r_done)
                mm(pz, identb[:], xp_all(par, Z, s), True, False)
                for wpart in range(PARTS):
                    for half in range(KC):
                        for k in range(KC):
                            i = mm(pz[:, half], whp[:, wpart, Z, k, half * P:(half + 1) * P], hist_all(bp, k, bs),
                                   False, wpart == PARTS - 1)
                i.then_inc(z_done, 1)
                inject(ph, par, H, s)

            def step_end(m, par, s):
                n = step_count(m, s)
                recur(ph, H, [(q, n, lambda k, part=part: rhv[:, part, k, 1::2])
                              for part, q in enumerate((rh_hi, rh_mid, rh_low))], h_done)
                if s + 1 < STEPS:
                    inject(pr, par, R, s + 1)

            def between(m, par, s, has_y, has_l23, has_l0):
                m1, m2 = later(m, 1), later(m, 2)
                q = 1 - par
                if has_l23:
                    if s == 0:
                        mid_base(m1)
                    if s == 1:
                        mid_low(m1)
                    if s == 3:
                        up_base(m1)
                    if s == 4:
                        up_low(m1)
                    if s == 5:
                        pe.wait_ge(x3_done, count(m1, 1))
                        project(q, 0, R, 0)
                    if s == 6:
                        project(q, 0, R, 1)
                        project(q, 1, Z, 0)
                        project(q, 1, Z, 1, projrz_done)
                    if s == 9:
                        pe.wait_ge(xprz_done, count(m1, 1))
                        project(q, 0, H, 0)
                        project(q, 0, H, 1, projh_done)
                if has_y and s == 1:
                    y_out(later(m, -1), q, True)
                if has_l0:
                    if s == 2:
                        if has_y:
                            pe.wait_ge(out_done, count(later(m, -1), 1))
                        scores(m2, par)
                        up_chunks(A1, sw1, par, (0, 1), a1_done, False)
                    if s == 4:
                        up_chunks(A1, sw1, par, (2, 3), a1_done, True)
                    if s == 5:
                        up_chunks(A3, sw3, par, (0, 1), a3_done, False)
                    if s == 7:
                        up_chunks(A3, sw3, par, (2, 3), a3_done, True)
                        up_chunks(E47, rw1, par, (4,), ex47_done, False)
                    if s == 8:
                        up_chunks(E47, rw1, par, (5, 6, 7), ex47_done, True)
                    if s == 9:
                        pe.wait_ge(sa_done, count(m2, 1))
                        up_chunks(A1, rw1, par, (0,), ex03_done, False)
                    if s == 10:
                        up_chunks(A1, rw1, par, (1, 2, 3), ex03_done, True)
                    if s == 11:
                        spread_gates(m2, D4, (4, 5, 6, 7), cb47_done, True)
                        pe.wait_ge(gs_done, count(m2, 1))
                        spread_gates(m2, A3, (0, 1), cb03_done, False)
                    if s == 12:
                        spread_gates(m2, A3, (2, 3), cb03_done, True)
                        if has_l23:
                            pe.wait_ge(xph_done, count(m1, 1))
                        l0_out(0, "s", (0, 1, 2, 3), start=True)
                    if s == 13:
                        pe.wait_ge(ge47_done, count(m2, 1))
                        l0_out(0, "r", (4, 5, 6, 7))
                        l0_out(1, "s", (0, 1))
                    if s == 14:
                        l0_out(1, "s", (2, 3))
                        l0_out(1, "r", (4, 5, 6, 7))
                    if s == 15:
                        pe.wait_ge(ge03_done, count(m2, 1))
                        l0_out(0, "r", (0, 1, 2, 3))
                        l0_out(1, "r", (0, 1, 2, 3), done=l0_done)

            def body(m, par, has_y, has_l23, has_l0):
                for s in range(STEPS):
                    step(m, par, s, s == 0)
                    step_end(m, par, s)
                    between(m, par, s, has_y, has_l23, has_l0)

            pe.wait_ge(cond_in, 32)
            pe.wait_ge(l0_in, 64)
            for k in range(KC):
                i = mm(A1[:, 0:EXPERTS], cond_tok[:, k], rtw[:, k], k == 0, k == KC - 1)
            i.then_inc(setup_pe, 1)
            pe.wait_ge(l1_in, 48)
            for half in range(KC):
                for k in range(KC):
                    i = mm(A3[:, half * B:(half + 1) * B], l1w1[:, k, half * P:(half + 1) * P], condT[:, k],
                           k == 0, k == KC - 1)
            i.then_inc(setup_pe, 1)
            pe.wait_ge(const_in, 64)
            pe.wait_ge(ready_dve, 1)
            for k in range(KC):
                i = mm(E47[:, k * B:(k + 1) * B], cn[:, k * P:(k + 1) * P], ident[0:B, 0:B], True, True)
            i.then_inc(setup_pe, 1)
            pe.wait_ge(ready_dve, 2)
            for half in range(KC):
                for k in range(KC):
                    i = mm(D4[:, half * B:(half + 1) * B], l1w2[:, k, half * P:(half + 1) * P], l1h[:, k],
                           k == 0, k == KC - 1)
            i.then_inc(setup_pe, 1)
            pe.wait_ge(ad_in, 32)
            pe.wait_ge(ready_dve, 3)
            for half in range(KC):
                for k in range(KC):
                    i = mm(E5[:, half * B:(half + 1) * B], aw1[:, k, half * P:(half + 1) * P], cT[:, k],
                           k == 0, k == KC - 1)
            i.then_inc(setup_pe, 1)

            def l0_whole_a(m, par):
                scores(m, par)
                up_chunks(A1, sw1, par, range(4), a1_done, True)
                up_chunks(A3, sw3, par, range(4), a3_done, True)
                pe.wait_ge(l0r_in, 48)
                up_chunks(E47, rw1, par, range(4, 8), ex47_done, True)
                pe.wait_ge(sa_done, count(m, 1))
                up_chunks(A1, rw1, par, range(0, 4), ex03_done, True)

            def l0_whole_b(m, par):
                spread_gates(m, D4, (4, 5, 6, 7), cb47_done, True)
                pe.wait_ge(gs_done, count(m, 1))
                spread_gates(m, A3, (0, 1, 2, 3), cb03_done, True)
                l0_out(0, "s", (0, 1, 2, 3), start=True)
                l0_out(1, "s", (0, 1, 2, 3))
                pe.wait_ge(ge47_done, count(m, 1))
                l0_out(0, "r", (4, 5, 6, 7))
                l0_out(1, "r", (4, 5, 6, 7))
                pe.wait_ge(ge03_done, count(m, 1))
                l0_out(0, "r", (0, 1, 2, 3))
                l0_out(1, "r", (0, 1, 2, 3), done=l0_done)

            pe.wait_ge(setup_dve, 10)
            l0_whole_a((0, 0), 0)
            pe.wait_ge(ad2_in, 32)
            pe.wait_ge(setup_act, 2)
            for c in range(ADAPT // 512):
                if c >= 3:
                    pe.wait_ge(wrow_dve, c - 2)
                p_ = (p_r, p_z, p_h)[c % 3]
                for k in range(KC):
                    i = mm(p_[0:B, :], ah[:, k], aw2[:, k, c * 512:(c + 1) * 512], k == 0, k == KC - 1)
                i.then_inc(adapt_pe, 1)
            l0_whole_b((0, 0), 0)
            pe.wait_ge(ready_dve, 4)
            for i_, src in enumerate((2, 1)):
                for k in range(KC):
                    i = mm(p_r[:, (i_ * KC + k) * BR:(i_ * KC + k + 1) * BR], low[:, src, k * P:(k + 1) * P],
                           ident[0:BR, 0:BR], True, True)
            i.then_inc(lowT_pe, 1)
            pe.wait_ge(ready_dve, 5)
            m0 = (0, 0)
            pe.wait_ge(l2_in, 32)
            mid_base(m0)
            l0_whole_a((0, 1), 1)
            mid_low(m0)
            up_base(m0)
            up_low(m0)
            pe.wait_ge(x3_done, 1)
            pe.wait_ge(wx_in, 16 * 3)
            project(0, 0, R, 0)
            project(0, 0, R, 1)
            project(0, 1, Z, 0)
            project(0, 1, Z, 1, projrz_done)
            pe.wait_ge(xprz_done, 1)
            project(0, 0, H, 0)
            project(0, 0, H, 1, projh_done)
            pe.wait_ge(xph_done, 1)
            l0_whole_b((0, 1), 1)
            pe.wait_ge(split_w, 9)
            blocks(pe, body)
            y_out((0, BLOCKS - 1), 1, True)

        @block.scalar
        def _(act):
            def func(o, i, f, **kw):
                return act.activation(o, i, f, **kw)

            def tanh_a1(m):
                act.wait_ge(a1_done, count(m, 1))
                func(sig1[:], A1[:, :], ACT.Tanh, scale=0.5).then_inc(a1_sig, 1)

            def gelu_experts(m, group, p_, ready, done):
                act.wait_ge(ready, count(m, 1))
                func(pe_e[:, group], p_[:, :], ACT.Gelu).then_inc(done, 1)

            def gelu_mid(m):
                act.wait_ge(mid_done, count(m, 1))
                func(g2[:], mid_ps, ACT.Gelu).then_inc(g2_done, 1)

            def evacuate(m, par, slot, g, ready, done=None):
                act.wait_ge(ready, count(m, 1))
                for half in range(KC):
                    i = func(xp[:, par, 0, g, half], proj_ps[:, slot, half], ACT.Identity, bias=bxh[:, g, half:half + 1])
                if done is not None:
                    i.then_inc(done, 1)

            def after(m, par, s, has_y, has_l23, has_l0):
                m1, m2 = later(m, 1), later(m, 2)
                q = 1 - par
                if has_l23:
                    if s == 1:
                        gelu_mid(m1)
                    if s == 7:
                        evacuate(m1, q, 0, R, projrz_done)
                    if s == 8:
                        evacuate(m1, q, 1, Z, projrz_done, xprz_done)
                    if s == 10:
                        evacuate(m1, q, 0, H, projh_done, xph_done)
                if has_l0:
                    if s == 5:
                        tanh_a1(m2)
                    if s == 9:
                        gelu_experts(m2, 1, E47, ex47_done, pe47_done)
                    if s == 11:
                        gelu_experts(m2, 0, A1, ex03_done, pe03_done)

            def body(m, par, has_y, has_l23, has_l0):
                for s in range(STEPS):
                    n = step_count(m, s)
                    act.wait_ge(r_done, n)
                    func(rg[:], pr, ACT.Tanh, scale=0.5).then_inc(rg_done, 1)
                    act.wait_ge(zsum_done, n)
                    func(zg[:], zsum[:], ACT.Tanh, scale=0.5).then_inc(zg_done, 1)
                    act.wait_ge(h_done, n)
                    func(ht[:], ph, ACT.Tanh).then_inc(ht_done, 1)
                    after(m, par, s, has_y, has_l23, has_l0)

            act.wait_ge(setup_dve, 6)
            func(l1sig[:], l1pre[:], ACT.Tanh, scale=0.5).then_inc(setup_act, 1)
            act.wait_ge(setup_pe, 5)
            for half in range(KC):
                i = func(ah[:, half], E5[:, half * B:(half + 1) * B], ACT.Gelu, bias=lnab[:, 2, half:half + 1])
            i.then_inc(setup_act, 1)
            act.wait_ge(setup_dve, 8)
            func(l1sig[:], l1pre[:], ACT.Tanh, scale=0.5).then_inc(setup_act, 1)
            m0, m1 = (0, 0), (0, 1)
            tanh_a1(m0)
            gelu_experts(m0, 1, E47, ex47_done, pe47_done)
            gelu_experts(m0, 0, A1, ex03_done, pe03_done)
            tanh_a1(m1)
            gelu_mid(m0)
            gelu_experts(m1, 1, E47, ex47_done, pe47_done)
            act.wait_ge(setup_dve, 10)
            evacuate(m0, 0, 0, R, projrz_done)
            evacuate(m0, 0, 1, Z, projrz_done, xprz_done)
            evacuate(m0, 0, 0, H, projh_done, xph_done)
            gelu_experts(m1, 0, A1, ex03_done, pe03_done)
            blocks(act, body)

        @block.vector
        def _(dve):
            def add_router_bias(m):
                dve.wait_ge(scores_done, count(m, 1))
                dve.scalar_tensor_tensor(score[:], score_ps, -1.0, tbias[:], ALU.mult, ALU.subtract)\
                   .then_inc(score_in, 1)

            def gate_op(m, k):
                if k == 0:
                    dve.wait_ge(score_exp, count(m, 1))
                    i = dve.tensor_scalar(exp1[:], expn[:], 1.0, None, ALU.add)
                else:
                    dve.wait_ge(gating, count(m, GATE_OPS, k - GATE_OPS))
                if k in (3, 4):
                    dve.memset(holder[:], 0.0)
                if k == 1:
                    i = dve.reciprocal(sg[:], exp1[:])
                if k == 2:
                    i = dve.tensor_tensor(sel[:], sg[:], rbias[:], ALU.add)
                if k == 3:
                    i = dve.max(top8[:], sel[:])
                if k == 4:
                    i = dve.max_index(idx[:], top8[:], sel[:])
                if k == 5:
                    i = dve.tensor_copy(idxf[:], idx[:, 0:2])
                if k == 6:
                    i = dve.tensor_scalar(first[:], iota[:], idxf[:, 0:1], None, ALU.is_equal)
                if k == 7:
                    i = dve.scalar_tensor_tensor(chosen[:], iota[:], idxf[:, 1:2], first[:], ALU.is_equal, ALU.add)
                if k == 8:
                    i = dve.scalar_tensor_tensor(ssel[:], sg[:], 1.0, chosen[:], ALU.mult, ALU.mult,
                                                 accum_out=den[:, 0:1])
                if k == 9:
                    dve.tensor_scalar(den[:, 1:2], den[:, 0:1], EPS_GATE, 2.0, ALU.is_gt, ALU.mult)
                    i = dve.tensor_scalar(den[:, 2:3], den[:, 0:1], EPS_GATE, None, ALU.add)
                if k == 10:
                    dve.tensor_scalar(den[:, 3:4], den[:, 1:2], -0.5, 1.0, ALU.mult, ALU.add)
                    i = dve.reciprocal(den[:, 2:3], den[:, 2:3])
                if k == 11:
                    i = dve.tensor_scalar(scaled[:], ssel[:], den[:, 2:3], den[:, 1:2], ALU.mult, ALU.mult)
                if k == 12:
                    i = dve.scalar_tensor_tensor(comb[:], chosen[:], den[:, 3:4], scaled[:], ALU.mult, ALU.add)
                i.then_inc(gating, 1)

            def silu_a1(m):
                dve.wait_ge(a1_sig, count(m, 1))
                dve.scalar_tensor_tensor(sa[:], sig1[:], 1.0, A1[:, :], ALU.add, ALU.mult).then_inc(sa_done, 1)

            def times_a3(m):
                dve.wait_ge(a3_done, count(m, 1))
                dve.wait_ge(sa_done, count(m, 1))
                dve.tensor_tensor(gs[:], sa[:], A3[:, :], ALU.mult).then_inc(gs_done, 1)

            def times_gate(m, group, p_, ready, mine, done):
                dve.wait_ge(ready, count(m, 1))
                dve.wait_ge(mine, count(m, 1))
                dve.tensor_tensor(ge[:, group], pe_e[:, group], p_[:, :], ALU.mult).then_inc(done, 1)

            def finish_l0(m, par):
                dve.wait_ge(l0_done, count(m, 1))
                dve.scalar_tensor_tensor(x1[:], l0_ps, 1.0 / 6.0, xt[:, par], ALU.mult, ALU.add).then_inc(x1_done, 1)

            def l1(m):
                dve.wait_ge(x1_done, count(m, 1))
                g = gate2[:].unsqueeze(2).to_broadcast([P, KC, STEPS, B])
                dve.tensor_tensor(x2[:].rearrange("p k (t b) -> p k t b", b=B),
                                  x1[:].rearrange("p k (t b) -> p k t b", b=B), g, ALU.mult).then_inc(x2_done, 1)

            def keep_own(m, dst, ready, done):
                dve.wait_ge(ready, count(m, 1))
                dve.tensor_tensor(dst[:], own[:], low_ps, ALU.mult).then_inc(done, 1)

            def finish_l2(m, par):
                dve.wait_ge(l2_done, count(m, 1))
                dve.scalar_tensor_tensor(x3[:, par], x2[:], 2.0, mid_ps, ALU.mult, ALU.add).then_inc(x3_done, 1)

            def split(par, part, gates, waits, done):
                for q, v in waits:
                    dve.wait_ge(q, v)
                a_, b_ = gates
                hi = xpv[:, par, part - 1, a_:b_].rearrange("p g k (t two) -> p (g k) t two", two=2)[:, :, :, 1]
                src = xp[:, par, part - 1, a_:b_].rearrange("p g k t -> p (g k) t")
                dst = xp[:, par, part, a_:b_].rearrange("p g k t -> p (g k) t")
                dve.tensor_tensor(dst, src, hi, ALU.subtract).then_inc(done, 1)

            def y_add(m, par):
                dve.wait_ge(y_done, count(m, 1))
                if not (type(m[0]) is int and m[1] == 0):
                    dve.wait_ge(stored, count(m, 16, -16))
                for half in range(KC):
                    i = dve.scalar_tensor_tensor(osb[:, half], y_ps[:, half], bq[:, half:half + 1], x3[:, par, half],
                                                 ALU.add, ALU.add)
                i.then_inc(out_done, 1)

            def early(m, par, s, has_y, has_l23, has_l0):
                m1, m2 = later(m, 1), later(m, 2)
                q = 1 - par
                if has_l23:
                    if s == 0:
                        finish_l0(m1, q)
                    if s == 1:
                        keep_own(m1, um, u_done, um_done)
                    if s == 4:
                        keep_own(m1, vm, v_done, vm_done)
                    if s == 5:
                        finish_l2(m1, q)
                    if s == 9:
                        split(q, 1, (Z, H), [(xprz_done, count(m1, 1))], rz_mid)
                    if s == 11:
                        split(q, 2, (Z, H), [(rz_mid, count(m1, 1))], rz_low)
                if has_y and s == 2:
                    y_add(later(m, -1), q)
                if has_l0:
                    if s == 3:
                        add_router_bias(m2)
                    if s == 4:
                        gate_op(m2, 0)
                    if s == 6:
                        silu_a1(m2)
                    if s == 5:
                        gate_op(m2, 2)
                    if s == 7:
                        gate_op(m2, 6)
                    if s == 8:
                        times_a3(m2)
                    if s == 10:
                        gate_op(m2, 11)
                    if s == 12:
                        times_gate(m2, 1, D4, cb47_done, pe47_done, ge47_done)
                    if s == 14:
                        times_gate(m2, 0, A3, cb03_done, pe03_done, ge03_done)

            def late(m, par, s, has_y, has_l23, has_l0):
                m1, m2 = later(m, 1), later(m, 2)
                q = 1 - par
                if has_l23:
                    if s == 0:
                        l1(m1)
                    if s == 13:
                        split(q, 1, (H, H + 1), [(xph_done, count(m1, 1))], h_mid_x)
                    if s == 14:
                        split(q, 2, (H, H + 1), [(h_mid_x, count(m1, 1))], h_low_x)
                if has_l0:
                    for at, k in ((4, 1), (5, 3), (6, 4), (6, 5), (7, 7), (8, 8), (9, 9), (9, 10), (10, 12)):
                        if s == at:
                            gate_op(m2, k)

            def body(m, par, has_y, has_l23, has_l0):
                for s in range(STEPS):
                    n = step_count(m, s)
                    bp, bs = before(par, s)
                    old = hist[:, bp, 0, :, bs * B:(bs + 1) * B]
                    cols = slice(s * B, (s + 1) * B)
                    hi = slice(2 * s * B + 1, 2 * (s + 1) * B, 2)
                    early(m, par, s, has_y, has_l23, has_l0)
                    dve.wait_ge(rg_done, n)
                    dve.scalar_tensor_tensor(rh[:, 0], rg[:], 1.0, old, ALU.add, ALU.mult).then_inc(rh_hi, 1)
                    dve.wait_ge(rh_hi, n)
                    dve.tensor_tensor(rh[:, 1], rh[:, 0], rhv[:, 0, :, 1::2], ALU.subtract).then_inc(rh_mid, 1)
                    dve.wait_ge(rh_mid, n)
                    dve.tensor_tensor(rh[:, 2], rh[:, 1], rhv[:, 1, :, 1::2], ALU.subtract).then_inc(rh_low, 1)
                    dve.wait_ge(z_done, n)
                    dve.tensor_reduce(zsum[:], pz.rearrange("p k a c -> p k c a"), AX_X, ALU.add).then_inc(zsum_done, 1)
                    late(m, par, s, has_y, has_l23, has_l0)
                    dve.wait_ge(zg_done, n)
                    dve.scalar_tensor_tensor(zh[:], zg[:], 1.0, old, ALU.add, ALU.mult).then_inc(zh_done, 1)
                    dve.wait_ge(ht_done, n)
                    dve.scalar_tensor_tensor(fresh[:], zg[:], -1.0, ht[:], ALU.add, ALU.mult).then_inc(fresh_done, 1)
                    dve.wait_ge(zh_done, n)
                    dve.wait_ge(fresh_done, n)
                    dve.scalar_tensor_tensor(hist[:, par, 0, :, cols], zh[:], 0.5, fresh[:], ALU.mult, ALU.subtract)\
                       .then_inc(st_hi, 1)
                    dve.wait_ge(st_hi, n + 1)
                    dve.tensor_tensor(hist[:, par, 1, :, cols], hist[:, par, 0, :, cols], histv[:, par, 0, :, hi],
                                      ALU.subtract).then_inc(st_mid, 1)
                    dve.wait_ge(st_mid, n + 1)
                    dve.tensor_tensor(hist[:, par, 2, :, cols], hist[:, par, 1, :, cols], histv[:, par, 1, :, hi],
                                      ALU.subtract).then_inc(st_low, 1)

            c_ = [0]

            def link(i):
                c_[0] += 1
                i.then_inc(setup_dve, 1)
                dve.wait_ge(setup_dve, c_[0])

            dve.wait_ge(cond_in, 32)
            link(dve.bn_stats(stats[:], cond[:]))
            link(dve.bn_aggr(meanvar[:], stats[:]))
            dve.memset(lnv[:, 1:2], -0.5)
            link(dve.tensor_scalar(lnv[:, 0:1], meanvar[:, 1:2], EPS_LN, None, ALU.add))
            dve.wait_ge(setup_pool, 1)
            dve.tensor_scalar(cn[:], cond[:], meanvar[:, 0:1], lnv[:, 2:3], ALU.subtract, ALU.mult).then_inc(ready_dve, 1)
            dve.wait_ge(setup_pe, 1)
            link(dve.tensor_copy(tbias[:], A1[:, 0:EXPERTS]))
            dve.wait_ge(setup_pe, 2)
            dve.wait_ge(l1_in, 48)
            for half in range(KC):
                link(dve.tensor_scalar(l1pre[:, half], A3[:, half * B:(half + 1) * B], l1b[:, 0, half:half + 1], None,
                                       ALU.add))
            dve.wait_ge(setup_act, 1)
            dve.scalar_tensor_tensor(l1h[:], l1sig[:], 1.0, l1pre[:], ALU.add, ALU.mult).then_inc(ready_dve, 1)
            dve.wait_ge(setup_pe, 3)
            dve.wait_ge(ad_in, 32)
            for k in range(KC):
                i = dve.tensor_scalar(cT[:, k], E47[:, k * B:(k + 1) * B], lnab[:, 0, k:k + 1], lnab[:, 1, k:k + 1],
                                      ALU.mult, ALU.add)
            i.then_inc(ready_dve, 1)
            dve.wait_ge(setup_pe, 4)
            for half in range(KC):
                link(dve.tensor_scalar(l1pre[:, half], D4[:, half * B:(half + 1) * B], 0.5, l1b[:, 1, half:half + 1],
                                       ALU.mult, ALU.add))
            dve.wait_ge(setup_act, 3)
            link(dve.tensor_scalar(gate2[:], l1sig[:], 0.5, 2.5, ALU.mult, ALU.add))
            dve.wait_ge(bias_in, 16 * 3)
            dve.tensor_copy(identb[:], ident[:])
            link(dve.tensor_tensor(bxh[:], bx[:], bh[:], ALU.add))

            def gates_whole(m):
                for k in range(GATE_OPS):
                    gate_op(m, k)

            def l0_whole_a(m):
                add_router_bias(m)
                gates_whole(m)
                silu_a1(m)
                times_a3(m)

            def l0_whole_b(m):
                times_gate(m, 1, D4, cb47_done, pe47_done, ge47_done)
                times_gate(m, 0, A3, cb03_done, pe03_done, ge03_done)

            m0, m1 = (0, 0), (0, 1)
            dve.wait_ge(const_in, 64)
            l0_whole_a(m0)
            for c in range(ADAPT // 512):
                dve.wait_ge(adapt_pe, c + 1)
                dve.tensor_copy(wrow[:, c * 512:(c + 1) * 512], (p_r, p_z, p_h)[c % 3][0:B, :]).then_inc(wrow_dve, 1)
            last = slice((STEPS - 1) * B, STEPS * B)
            lhi = slice(2 * (STEPS - 1) * B + 1, 2 * STEPS * B, 2)
            dve.tensor_scalar(hist[:, 1, 0, :, last], condT, 2.0, None, ALU.mult).then_inc(st_hi, 1)
            dve.wait_ge(st_hi, 1)
            dve.tensor_tensor(hist[:, 1, 1, :, last], hist[:, 1, 0, :, last], histv[:, 1, 0, :, lhi],
                              ALU.subtract).then_inc(st_mid, 1)
            dve.wait_ge(st_mid, 1)
            dve.tensor_tensor(hist[:, 1, 2, :, last], hist[:, 1, 1, :, last], histv[:, 1, 1, :, lhi],
                              ALU.subtract).then_inc(st_low, 1)
            l0_whole_b(m0)
            finish_l0(m0, 0)
            l1(m0)
            dve.wait_ge(low_in, 4 * B * 16)
            dve.wait_ge(abias_in, 16 * B)
            dve.tensor_tensor(low[:], low[:], abias[:], ALU.add).then_inc(ready_dve, 1)
            dve.wait_ge(lowT_pe, 1)
            dve.tensor_copy(a2b1[:], p_r[:, 0:2 * KC * BR].rearrange("p (i k c) -> p i k c", i=2, k=KC))\
               .then_inc(ready_dve, 1)
            keep_own(m0, um, u_done, um_done)
            l0_whole_a(m1)
            keep_own(m0, vm, v_done, vm_done)
            finish_l2(m0, 0)
            split(0, 1, (Z, H), [(xprz_done, 1)], rz_mid)
            split(0, 2, (Z, H), [(rz_mid, 1)], rz_low)
            split(0, 1, (H, H + 1), [(xph_done, 1)], h_mid_x)
            split(0, 2, (H, H + 1), [(h_mid_x, 1)], h_low_x)
            l0_whole_b(m1)
            blocks(dve, body)
            y_add((0, BLOCKS - 1), 1)


def kernel(**inputs):
    import concourse.bacc as _bacc
    from concourse.bass_utils import run_bass_kernel_spmd as _run

    f = {k: np.asarray(v) for k, v in inputs.items()}

    def rows(w):
        return np.ascontiguousarray(w.reshape(-1, P, w.shape[-1]).transpose(1, 0, 2))

    def vec(v):
        return v.reshape(KC, P).T

    g3 = ("z", "r", "h")
    L0, L1, L2, L3 = ("L0_cond_", "L1_cond_", "L2_cond_", "L3_cond_")
    w2 = f[L2 + "W2"].reshape(D, 4, D, RANK).transpose(0, 1, 3, 2).reshape(D, ADAPT)
    tok = np.arange(TOK)
    arrays = {
        "xT": rows(f["x"].transpose(2, 1, 0).reshape(D, T * B)),
        "cond_tok": rows(f["cond_1024"].T[:, tok % B]),
        "cond": f["cond_1024"],
        "sw1": rows(f[L0 + "sw1"].T), "sw3": rows(f[L0 + "sw3"].T), "sw2": rows(f[L0 + "sw2"].T),
        "rw1": rows(f[L0 + "rw1"].reshape(EXPERTS * HR, D).T),
        "rw2": rows(f[L0 + "rw2"].transpose(0, 2, 1).reshape(EXPERTS * HR, D)),
        "rw": rows(f[L0 + "router_w"].T), "rtw": rows(f[L0 + "router_t_w"].T), "rbias": f[L0 + "router_bias"],
        "l1w1": rows(f[L1 + "W1"].T), "l1w2": rows(f[L1 + "W2"].T),
        "l1b": np.stack([vec(f[L1 + "b1"]), vec(f[L1 + "b2"])], 1),
        "down": rows(f[L2 + "base_down"]), "up": rows(f[L2 + "base_up"].T),
        "aw1": rows(f[L2 + "W1"]), "aw2": rows(w2),
        "lnab": np.stack([vec(f[L2 + n]) for n in ("ln_gamma", "ln_beta", "bias1")], 1),
        "abias": f[L2 + "bias2"].reshape(4, D, RANK).transpose(2, 0, 1),
        "wx": np.stack([rows(f[L3 + "Wx" + g].T) for g in g3]),
        "wh": np.stack([rows(f[L3 + "Wh" + g].T) for g in g3]),
        "wq": rows(f[L3 + "Whq"].T),
        "bx": np.stack([vec(f[L3 + "bx" + g]) for g in g3], 1),
        "bh": np.stack([vec(f[L3 + "bh" + g]) for g in g3], 1),
        "bq": vec(f[L3 + "bhq"]),
        "ident": np.eye(P, dtype=np.float32),
        "iota": np.tile(np.arange(EXPERTS, dtype=np.float32), (P, 1)),
        "own": (np.arange(BR)[:, None] // RANK == tok[None] % B).astype(np.float32),
    }
    nc = _bacc.Bacc("TRN2", target_bir_lowering=False, num_devices=1)
    feeds, handles = {}, {}
    for name, v in arrays.items():
        v = np.ascontiguousarray(v)
        feeds[f"in_{name}"] = v
        handles[name] = nc.dram_tensor(f"in_{name}", v.shape, mybir.dt.from_np(v.dtype), kind="ExternalInput").ap()
    out = nc.dram_tensor("out_0", (P, KC, T * B), F32, kind="ExternalOutput").ap()
    build(nc, handles, out)
    r = _run(nc, [feeds], core_ids=[0])
    got = r.results[0]["out_0"]
    return np.ascontiguousarray(got.reshape(P, KC, T, B).transpose(3, 2, 1, 0).reshape(B, T, D))
```

```python
from contextlib import ExitStack

import numpy as np
import concourse.bass as bass
from concourse import mybir

ALU = mybir.AluOpType
ACT = mybir.ActivationFunctionType
F32 = mybir.dt.float32
BF16 = mybir.dt.bfloat16
F16 = mybir.dt.float16
U32 = mybir.dt.uint32
AX_X = mybir.AxisListType.X
AX_XY = mybir.AxisListType.XY

P = 128
B, T, D = 8, 512, 256
KC = D // P
TOK = P
STEPS = TOK // B
BLOCKS = T // STEPS
HS = 512
EXPERTS, HR = 8, 128
RANK = 8
BR = B * RANK
ADAPT = 4 * RANK * D
XPARTS = 3
HPARTS = 2
W_TOP, S_TOP = 14, 12
GATE_OPS = 13
Z, R, H = range(3)
EPS_GATE, EPS_LN = 1e-9, 1e-5
LEAST_PEAK = 2.0 ** -40
EXPONENT_BITS = 0x7F800000


def count(m, per, extra=0):
    return m[0] * (2 * per) + ((m[1] + 1) * per + extra)


def pair_count(m, per):
    return m[0] * per + (m[1] // 2 + 1) * per


def step_count(m, s):
    return m[0] * (2 * STEPS) + (m[1] * STEPS + s + 1)


def token_start(m):
    return m[0] * (2 * TOK) + m[1] * TOK


def build(nc, a, out):
    with ExitStack() as ctx:
        def sb(name, shape, dt=F32):
            return ctx.enter_context(nc.sbuf_tensor(name, shape, dt))

        def ps(name, shape=(P, 512), dt=F32):
            return ctx.enter_context(nc.psum_tensor(name, list(shape), dt))

        def sem(name):
            return ctx.enter_context(nc.semaphore(name))

        sw1 = sb("sw1", [P, KC, HS])
        sw3 = sb("sw3", [P, KC, HS])
        sw2 = sb("sw2", [P, HS // P, D])
        rw1 = sb("rw1", [P, KC, EXPERTS * HR])
        rw2 = sb("rw2", [P, EXPERTS, D])
        rw = sb("rw", [P, KC, EXPERTS])
        rtw = sb("rtw", [P, KC, EXPERTS])
        rbias = sb("rbias", [P, EXPERTS])
        l1w1 = sb("l1w1", [P, KC, D])
        l1w2 = sb("l1w2", [P, KC, D])
        l1b = sb("l1b", [P, 2, KC])
        down = sb("down", [P, KC, D])
        up = sb("up", [P, KC, D])
        aw1 = sb("aw1", [P, KC, D])
        aw2 = sb("aw2", [P, KC, ADAPT])
        lnab = sb("lnab", [P, 3, KC])
        abias = sb("abias", [BR, 4, D])
        wx = sb("wx", [P, 3, KC, D])
        wh = sb("wh", [P, 3, KC, D])
        wrest = sb("wrest", [P, 3, KC, D])
        whp = sb("whp", [P, HPARTS, 3, KC, D], F16)
        wq = sb("wq", [P, KC, D])
        wqh = sb("wqh", [P, KC, D])
        bx = sb("bx", [P, 3, KC])
        bh = sb("bh", [P, 3, KC])
        bxh = sb("bxh", [P, 3, KC])
        bq = sb("bq", [P, KC])
        ident = sb("ident", [P, P])
        identb = sb("identb", [P, P], BF16)
        iota = sb("iota", [P, EXPERTS])
        own = sb("own", [BR, TOK])
        cond_tok = sb("cond_tok", [P, KC, TOK])
        condT = cond_tok[:, :, 0:B]
        cond = sb("cond", [B, D])

        tbias = sb("tbias", [P, EXPERTS])
        l1pre = sb("l1pre", [P, KC, B])
        l1sig = sb("l1sig", [P, KC, B])
        l1h = sb("l1h", [P, KC, B])
        gate2 = sb("gate2", [P, KC, B])
        stats = sb("stats", [B, 6])
        meanvar = sb("meanvar", [B, 2])
        lnv = sb("lnv", [B, 3])
        cn = sb("cn", [B, D])
        cT = sb("cT", [P, KC, B])
        ah = sb("ah", [P, KC, B])
        wrow = sb("wrow", [B, ADAPT])
        low = sb("low", [BR, 4, D])
        a2b1 = sb("a2b1", [P, 2, KC, BR])

        xt = sb("xt", [P, 2, KC, TOK])
        holder = sb("holder", [P, 1])
        score = sb("score", [P, EXPERTS])
        euler = sb("euler", [P, EXPERTS])
        expn = sb("expn", [P, EXPERTS])
        exp1 = sb("exp1", [P, EXPERTS])
        sg = sb("sg", [P, EXPERTS])
        sel = sb("sel", [P, EXPERTS])
        top8 = sb("top8", [P, 8])
        idx = sb("idx", [P, 8], U32)
        idxf = sb("idxf", [P, 2])
        first = sb("first", [P, EXPERTS])
        chosen = sb("chosen", [P, EXPERTS])
        ssel = sb("ssel", [P, EXPERTS])
        den = sb("den", [P, 4])
        scaled = sb("scaled", [P, EXPERTS])
        comb = sb("comb", [P, EXPERTS])
        sig1 = sb("sig1", [P, HS])
        sa = sb("sa", [P, HS])
        gs = sb("gs", [P, HS])
        pe_e = sb("pe_e", [P, 2, 4 * TOK])
        ge = sb("ge", [P, 2, 4 * TOK])
        x1 = sb("x1", [P, KC, TOK])
        x2 = sb("x2", [P, KC, TOK])
        g2 = sb("g2", [P, KC, TOK])
        um = sb("um", [BR, TOK])
        vm = sb("vm", [BR, TOK])
        x3 = sb("x3", [P, 2, KC, TOK])
        xp = aw2[:, 0, 0:2 * XPARTS * 3 * KC * TOK].rearrange("p (u a g k t) -> p u a g k t", u=2, a=XPARTS, g=3, k=KC)
        hist = aw2[:, 1, 0:2 * KC * TOK].rearrange("p (u k t) -> p u k t", u=2, k=KC)
        state = sb("state", [P, KC, HPARTS, B], F16)
        rh = sb("rh", [P, KC, B])
        rhp = sb("rhp", [P, KC, HPARTS, B], F16)
        peak = sb("peak", [P, 4])
        peak4 = sb("peak4", [4, 1])
        peakd = sb("peakd", [4, 4])
        ones4 = sb("ones4", [4, P])
        power = sb("power", [P, 4])
        inv = sb("inv", [P, 4])
        wscale = sb("wscale", [P, 3])
        sscale = sb("sscale", [P, 1])
        xscale = sb("xscale", [P, 3])
        unscale = sb("unscale", [P, 3])
        qscale = sb("qscale", [P, 1])
        sscale2 = sb("sscale2", [P, 1])
        zm = sb("zm", [P, KC, B])
        rg = sb("rg", [P, KC, B])
        zg = sb("zg", [P, KC, B])
        zsum = sb("zsum", [P, KC, B])
        zh = sb("zh", [P, KC, B])
        ht = sb("ht", [P, KC, B])
        fresh = sb("fresh", [P, KC, B])
        osb = sb("osb", [P, KC, TOK])

        xpv = xp.bitcast(BF16)

        def xp_part(par, part, g, s):
            return xpv[:, par, part, g, :, 2 * s * B + 1:2 * (s + 1) * B:2]

        def before(par, s):
            return (par, s - 1) if s else (1 - par, STEPS - 1)

        p_r, p_z, p_h = ps("p_r"), ps("p_z"), ps("p_h")
        bank = [ps(f"bank{i}") for i in range(5)]
        A1, A3, E47, D4, E5 = bank
        pr = p_r[:, 0:KC * B].rearrange("p (k c) -> p k c", k=KC)
        ph = p_h[:, 0:KC * B].rearrange("p (k c) -> p k c", k=KC)
        pz = p_z[:, 0:KC * XPARTS * B].rearrange("p (k a c) -> p k a c", k=KC, a=XPARTS)
        y_ps = D4[:, 0:KC * TOK].rearrange("p (k t) -> p k t", k=KC)
        score_ps = D4[:, KC * TOK:KC * TOK + EXPERTS]
        l0_ps = E5[:, 0:KC * TOK].rearrange("p (k t) -> p k t", k=KC)
        mid_ps = E5[:, 0:KC * TOK].rearrange("p (k t) -> p k t", k=KC)
        low_ps = E5[0:BR, KC * TOK:(KC + 1) * TOK]
        proj_ps = E5[:, :].rearrange("p (g k t) -> p g k t", g=2, k=KC)

        cond_in, l1_in, ad_in, ad2_in, l0_in, l0r_in, l2_in, rec_in, const_in, wx_in = (
            sem(n) for n in ("cond_in", "l1_in", "ad_in", "ad2_in", "l0_in", "l0r_in", "l2_in", "rec_in",
                             "const_in", "wx_in"))
        abias_in, bias_in, wq_in, setup_pool, peaks_dve, peaks_pe, scales_done = (
            sem(n) for n in ("abias_in", "bias_in", "wq_in", "setup_pool", "peaks_dve", "peaks_pe", "scales_done"))
        x_in = [sem("x_in0"), sem("x_in1")]
        stored = sem("stored")
        low_in = sem("low_in")
        split_w, setup_pe, setup_act, setup_dve, wrow_dve, adapt_pe, lowT_pe, ready_dve = (
            sem(n) for n in ("split_w", "setup_pe", "setup_act", "setup_dve", "wrow_dve", "adapt_pe", "lowT_pe",
                             "ready_dve"))
        names = ("scores_done", "a1_done", "a3_done", "ex47_done", "ex03_done", "cb47_done", "cb03_done", "l0_done",
                 "u_done", "mid_done", "v_done", "l2_done", "projrz_done", "projh_done", "y_done",
                 "score_exp", "a1_sig", "xprz_done", "xph_done",
                 "score_in", "gating", "sa_done", "gs_done", "pe47_done", "ge47_done", "pe03_done", "ge03_done",
                 "x1_done", "x2_done", "um_done", "g2_done", "vm_done", "x3_done", "rz_mid", "rz_low", "h_mid_x",
                 "h_low_x", "out_done")
        (scores_done, a1_done, a3_done, ex47_done, ex03_done, cb47_done, cb03_done, l0_done,
         u_done, mid_done, v_done, l2_done, projrz_done, projh_done, y_done,
         score_exp, a1_sig, xprz_done, xph_done,
         score_in, gating, sa_done, gs_done, pe47_done, ge47_done, pe03_done, ge03_done,
         x1_done, x2_done, um_done, g2_done, vm_done, x3_done, rz_mid, rz_low, h_mid_x,
         h_low_x, out_done) = (sem(n) for n in names)
        (r_done, z_done, h_done, rg_done, zg_done, ht_done, rh_hi, rh_all, rh_low, zsum_done, zm_done,
         fresh_done, st_hi, st_all, st_low) = (
            sem(n) for n in ("r_done", "z_done", "h_done", "rg_done", "zg_done", "ht_done", "rh_hi", "rh_all",
                             "rh_low", "zsum_done", "zm_done", "fresh_done", "st_hi", "st_all", "st_low"))

        block = ctx.enter_context(nc.Block())

        def blocks(eng, body):
            body((0, 0), 0, False, True, True)
            with eng.Fori(0, (BLOCKS - 4) // 2) as j:
                body((j, 1), 1, True, True, True)
                body((j, 2), 0, True, True, True)
            body((0, BLOCKS - 3), 1, True, True, True)
            body((0, BLOCKS - 2), 0, True, True, False)
            body((0, BLOCKS - 1), 1, True, False, False)

        def later(m, d):
            return (m[0], m[1] + d)

        @block.sync
        def _(sp):
            sp.dma_start(cond_tok[:], a["cond_tok"]).then_inc(cond_in, 16)
            sp.dma_start(cond[:], a["cond"]).then_inc(cond_in, 16)
            sp.dma_start(rw[:], a["rw"]).then_inc(l0_in, 16)
            sp.dma_start(rtw[:], a["rtw"]).then_inc(l0_in, 16)
            sp.dma_start(sw1[:], a["sw1"]).then_inc(l0_in, 16)
            sp.dma_start(aw1[:], a["aw1"]).then_inc(ad_in, 16)
            sp.dma_start(lnab[:], a["lnab"]).then_inc(ad_in, 16)
            sp.dma_start(sw3[:], a["sw3"]).then_inc(l0_in, 16)
            sp.dma_start(rw1[:], a["rw1"]).then_inc(l0r_in, 16)
            sp.dma_start(sw2[:], a["sw2"]).then_inc(l0r_in, 16)
            sp.dma_start(rw2[:], a["rw2"]).then_inc(l0r_in, 16)
            for k in range(KC):
                sp.dma_start(aw2[:, k], a["aw2"][:, k], max_dma_last_dim=8192).then_inc(ad2_in, 16)
            sp.dma_start(down[:], a["down"]).then_inc(l2_in, 16)
            sp.dma_start(up[:], a["up"]).then_inc(l2_in, 16)
            for g in range(3):
                sp.dma_start(wx[:, g], a["wx"][g]).then_inc(wx_in, 16)
            sp.dma_start(wq[:], a["wq"]).then_inc(wq_in, 16)
            for i in range(4):
                sp.wait_ge(wrow_dve, 4 * (i + 1))
                for b in range(B):
                    src = wrow[b:b + 1, i * RANK * D:(i + 1) * RANK * D].rearrange("b (r d) -> b r d", r=RANK)
                    sp.dma_start(low[b * RANK:(b + 1) * RANK, i, :], src).then_inc(low_in, 16)

        @block.gpsimd
        def _(pool):
            pool.dma_start(xt[:, 0], a["xT"][:, :, 0:TOK]).then_inc(x_in[0], 16)
            pool.dma_start(ident[:], a["ident"]).then_inc(const_in, 16)
            pool.dma_start(iota[:], a["iota"]).then_inc(const_in, 16)
            pool.dma_start(own[:], a["own"]).then_inc(const_in, 16)
            pool.dma_start(rbias[:], a["rbias"].partition_broadcast(P)).then_inc(const_in, 16)
            pool.dma_start(xt[:, 1], a["xT"][:, :, TOK:2 * TOK]).then_inc(x_in[1], 16)
            for g in range(3):
                pool.dma_start(wh[:, g], a["wh"][g]).then_inc(rec_in, 16)
            pool.dma_start(l1w1[:], a["l1w1"]).then_inc(l1_in, 16)
            pool.dma_start(l1w2[:], a["l1w2"]).then_inc(l1_in, 16)
            pool.dma_start(l1b[:], a["l1b"]).then_inc(l1_in, 16)
            pool.dma_start(bx[:], a["bx"]).then_inc(bias_in, 16)
            pool.dma_start(bh[:], a["bh"]).then_inc(bias_in, 16)
            pool.dma_start(bq[:], a["bq"]).then_inc(bias_in, 16)
            for b in range(B):
                pool.dma_start(abias[b * RANK:(b + 1) * RANK], a["abias"]).then_inc(abias_in, 16)
            pool.wait_ge(setup_dve, 3)
            pool.tensor_tensor(lnv[:, 2:3], lnv[:, 0:1], lnv[:, 1:2], ALU.pow).then_inc(setup_pool, 1)
            def exp_scores(m):
                pool.wait_ge(score_in, count(m, 1))
                pool.tensor_tensor(expn[:], euler[:], score[:], ALU.pow).then_inc(score_exp, 1)

            pool.memset(euler[:], float(np.e)).then_inc(setup_pool, 1)
            pool.wait_ge(setup_pool, 2)
            exp_scores((0, 0))
            pool.wait_ge(scales_done, 1)
            for g in range(3):
                pool.tensor_scalar(wrest[:, g], wh[:, g], wscale[:, g:g + 1], None, ALU.mult).then_inc(split_w, 1)
            pool.wait_ge(split_w, 3)
            pool.tensor_copy(whp[:, 0], wrest[:]).then_inc(split_w, 1)
            pool.wait_ge(split_w, 4)
            pool.tensor_tensor(whp[:, 1], wrest[:], whp[:, 0], ALU.subtract).then_inc(split_w, 1)
            pool.wait_ge(wq_in, 16)
            pool.tensor_scalar(wqh[:], wq[:], qscale[:], None, ALU.mult).then_inc(split_w, 1)

            def xcols(m):
                at = token_start(m)
                return at if type(at) is int else pool.snap(at)

            def load_x(at, par):
                pool.dma_start(xt[:, par], a["xT"][:, :, bass.ds(at, TOK)]).then_inc(x_in[par], 16)

            def store(m):
                at = xcols(m)
                pool.wait_ge(out_done, count(m, 1))
                pool.dma_start(out[:, :, bass.ds(at, TOK)], osb[:]).then_inc(stored, 16)

            pool.wait_ge(x1_done, 1)
            load_x(2 * TOK, 0)
            exp_scores((0, 1))

            def body(m, par, has_y, has_l23, has_l0):
                if has_l0 and not (type(m[0]) is int and m[1] + 3 >= BLOCKS):
                    x_block = xcols(later(m, 3))
                    pool.wait_ge(x1_done, count(later(m, 1), 1))
                    load_x(x_block, 1 - par)
                if has_l0:
                    exp_scores(later(m, 2))
                if has_y:
                    store(later(m, -1))

            blocks(pool, body)
            store((0, BLOCKS - 1))
            pool.wait_ge(stored, 16 * BLOCKS)


        @block.tensor
        def _(pe):
            def mm(o, w, x, start, stop):
                return pe.matmul(o, w, x, start=start, stop=stop, skip_group_check=True)

            def scores(m, par):
                pe.wait_ge(x_in[par], pair_count(m, 16))
                for k in range(KC):
                    i = mm(score_ps, xt[:, par, k], rw[:, k], k == 0, k == KC - 1)
                i.then_inc(scores_done, 1)

            def up_chunks(ps_, w, par, chunks, done, last):
                for c in chunks:
                    for k in range(KC):
                        i = mm(ps_[:, c % 4 * TOK:(c % 4 + 1) * TOK], w[:, k, c * P:(c + 1) * P], xt[:, par, k],
                               k == 0, k == KC - 1)
                if last:
                    i.then_inc(done, 1)

            def spread_gates(m, ps_, experts, done, last):
                pe.wait_ge(gating, count(m, GATE_OPS))
                for e in experts:
                    i = mm(ps_[:, e % 4 * TOK:(e % 4 + 1) * TOK], comb[:, e:e + 1].to_broadcast([P, P]), ident[:],
                           True, True)
                if last:
                    i.then_inc(done, 1)

            def l0_out(half, kind, chunks, start=False, done=None):
                for c in chunks:
                    w = sw2 if kind == "s" else rw2
                    g = gs[:, c * TOK:(c + 1) * TOK] if kind == "s" else ge[:, c // 4, c % 4 * TOK:(c % 4 + 1) * TOK]
                    i = mm(l0_ps[:, half], w[:, c, half * P:(half + 1) * P], g, start and c == chunks[0], False)
                if done is not None:
                    i.then_inc(done, 1)

            def mid_base(m):
                pe.wait_ge(x2_done, count(m, 1))
                for half in range(KC):
                    for k in range(KC):
                        mm(mid_ps[:, half], down[:, k, half * P:(half + 1) * P], x2[:, k],
                           half == 0 and k == 0, False)

            def low_in_rank(w, x, done):
                for k in range(KC):
                    i = mm(low_ps, a2b1[:, w, k], x[:, k], False, k == KC - 1)
                i.then_inc(done, 1)

            def mid_low(m):
                pe.wait_ge(um_done, count(m, 1))
                for half in range(KC):
                    i = mm(mid_ps[:, half], low[:, 3, half * P:(half + 1) * P], um[:], False, True)
                i.then_inc(mid_done, 1)

            def up_base(m):
                pe.wait_ge(g2_done, count(m, 1))
                for half in range(KC):
                    for k in range(KC):
                        mm(mid_ps[:, half], up[:, k, half * P:(half + 1) * P], g2[:, k], half == 0 and k == 0, False)

            def up_low(m):
                pe.wait_ge(vm_done, count(m, 1))
                for half in range(KC):
                    i = mm(mid_ps[:, half], low[:, 0, half * P:(half + 1) * P], vm[:], False, True)
                i.then_inc(l2_done, 1)

            def project(par, slot, g, half, done=None):
                for k in range(KC):
                    i = mm(proj_ps[:, slot, half], wx[:, g, k, half * P:(half + 1) * P], x3[:, par, k],
                           k == 0, k == KC - 1)
                if done is not None:
                    i.then_inc(done, 1)

            def y_out(m, par):
                pe.wait_ge(st_all, step_count(m, STEPS - 1) + 1)
                for half in range(KC):
                    for k in range(KC):
                        i = mm(y_ps[:, half], wqh[:, k, half * P:(half + 1) * P], hist[:, par, k], k == 0, k == KC - 1)
                i.then_inc(y_done, 1)

            def inject(p_, par, g, s, start=True):
                for part in range(XPARTS):
                    mm(p_, identb[:], xp_part(par, part, g, s), start and part == 0, False)

            def recur(p_, g, wpart, view, part, last=None):
                for half in range(KC):
                    for k in range(KC):
                        i = mm(p_[:, half], whp[:, wpart, g, k, half * P:(half + 1) * P], view[:, k, part], False,
                               last is not None)
                if last is not None:
                    i.then_inc(last, 1)

            def step(m, par, s):
                n = step_count(m, s)
                if s == 0:
                    pe.wait_ge(h_low_x, count(m, 1))
                    pe.wait_ge(rz_low, count(m, 1))
                    inject(pr, par, R, s)
                pe.wait_ge(st_hi, n)
                recur(pr, R, 0, state, 0)
                recur(pr, R, 1, state, 0)
                inject(ph, par, H, s)
                pe.wait_ge(st_low, n)
                recur(pr, R, 0, state, 1, r_done)
                mm(pz.rearrange("p k a c -> p a k c"), identb[:],
                   xpv[:, par, :, Z, :, 2 * s * B + 1:2 * (s + 1) * B:2], True, False)
                for wpart in range(HPARTS):
                    for half in range(KC):
                        for k in range(KC):
                            i = mm(pz[:, half, 0:HPARTS].rearrange("p a c -> p (a c)"),
                                   whp[:, wpart, Z, k, half * P:(half + 1) * P],
                                   state[:, k].rearrange("p a c -> p (a c)"), False, wpart == HPARTS - 1)
                i.then_inc(z_done, 1)

            def step_end(m, par, s):
                n = step_count(m, s)
                pe.wait_ge(rh_hi, n)
                recur(ph, H, 0, rhp, 0)
                recur(ph, H, 1, rhp, 0)
                if s + 1 < STEPS:
                    inject(pr, par, R, s + 1)
                pe.wait_ge(rh_low, n)
                recur(ph, H, 0, rhp, 1, h_done)

            def between_z_h(m, par, s, has_y, has_l23, has_l0):
                m1, m2 = later(m, 1), later(m, 2)
                if has_l0:
                    if s == 0:
                        scores(m2, par)
                    if s == 3:
                        up_chunks(A1, sw1, par, (2,), a1_done, False)
                    if s == 6:
                        up_chunks(A3, sw3, par, (3,), a3_done, True)
                    if s == 7:
                        up_chunks(E47, rw1, par, (4,), ex47_done, False)
                    if s == 8:
                        up_chunks(E47, rw1, par, (5,), ex47_done, False)
                    if s == 9:
                        pe.wait_ge(sa_done, count(m2, 1))
                        up_chunks(A1, rw1, par, (0,), ex03_done, False)
                    if s == 10:
                        up_chunks(A1, rw1, par, (1,), ex03_done, False)
                    if s == 11:
                        spread_gates(m2, D4, (4, 5), cb47_done, False)
                    if s == 12:
                        spread_gates(m2, A3, (2, 3), cb03_done, True)
                    if s == 13:
                        l0_out(0, "s", (2, 3))
                    if s == 14:
                        l0_out(1, "s", (2, 3))
                    if s == 15:
                        pe.wait_ge(ge03_done, count(m2, 1))
                        l0_out(0, "r", (0, 1))
                if has_l23:
                    if s == 1:
                        low_in_rank(0, x2, u_done)
                    if s == 2:
                        mid_low(m1)
                    if s == 4:
                        low_in_rank(1, g2, v_done)
                    if s == 5:
                        up_low(m1)

            def between_steps(m, par, s, has_y, has_l23, has_l0):
                m1, m2 = later(m, 1), later(m, 2)
                q = 1 - par
                if has_l23:
                    if s == 0:
                        mid_base(m1)
                    if s == 3:
                        up_base(m1)
                    if s == 6:
                        pe.wait_ge(x3_done, count(m1, 1))
                        project(q, 0, R, 0)
                        project(q, 0, R, 1)
                    if s == 7:
                        project(q, 1, Z, 0)
                        project(q, 1, Z, 1, projrz_done)
                    if s == 9:
                        pe.wait_ge(xprz_done, count(m1, 1))
                        project(q, 0, H, 0)
                        project(q, 0, H, 1, projh_done)
                if has_y and s == 1:
                    y_out(later(m, -1), q)
                if has_l0:
                    if s == 2:
                        up_chunks(A1, sw1, par, (0, 1), a1_done, False)
                    if s == 4:
                        up_chunks(A1, sw1, par, (3,), a1_done, True)
                        up_chunks(A3, sw3, par, (0,), a3_done, False)
                    if s == 5:
                        up_chunks(A3, sw3, par, (1, 2), a3_done, False)
                    if s == 8:
                        up_chunks(E47, rw1, par, (6, 7), ex47_done, True)
                    if s == 10:
                        up_chunks(A1, rw1, par, (2, 3), ex03_done, True)
                    if s == 11:
                        spread_gates(m2, D4, (6, 7), cb47_done, True)
                        pe.wait_ge(gs_done, count(m2, 1))
                        spread_gates(m2, A3, (0, 1), cb03_done, False)
                    if s == 12:
                        if has_l23:
                            pe.wait_ge(xph_done, count(m1, 1))
                        l0_out(0, "s", (0, 1), start=True)
                        l0_out(1, "s", (0, 1))
                    if s == 13:
                        pe.wait_ge(ge47_done, count(m2, 1))
                        l0_out(0, "r", (4, 5, 6, 7))
                    if s == 14:
                        l0_out(1, "r", (4, 5, 6, 7))
                    if s == 15:
                        l0_out(0, "r", (2, 3))
                        l0_out(1, "r", (0, 1, 2, 3), done=l0_done)

            def body(m, par, has_y, has_l23, has_l0):
                for s in range(STEPS):
                    step(m, par, s)
                    between_z_h(m, par, s, has_y, has_l23, has_l0)
                    step_end(m, par, s)
                    between_steps(m, par, s, has_y, has_l23, has_l0)

            pe.wait_ge(cond_in, 32)
            pe.wait_ge(l0_in, 64)
            for k in range(KC):
                i = mm(A1[:, 0:EXPERTS], cond_tok[:, k], rtw[:, k], k == 0, k == KC - 1)
            i.then_inc(setup_pe, 1)
            pe.wait_ge(l1_in, 48)
            for half in range(KC):
                for k in range(KC):
                    i = mm(A3[:, half * B:(half + 1) * B], l1w1[:, k, half * P:(half + 1) * P], condT[:, k],
                           k == 0, k == KC - 1)
            i.then_inc(setup_pe, 1)
            pe.wait_ge(const_in, 64)
            pe.wait_ge(ready_dve, 1)
            for k in range(KC):
                i = mm(E47[:, k * B:(k + 1) * B], cn[:, k * P:(k + 1) * P], ident[0:B, 0:B], True, True)
            i.then_inc(setup_pe, 1)
            pe.wait_ge(ready_dve, 2)
            for half in range(KC):
                for k in range(KC):
                    i = mm(D4[:, half * B:(half + 1) * B], l1w2[:, k, half * P:(half + 1) * P], l1h[:, k],
                           k == 0, k == KC - 1)
            i.then_inc(setup_pe, 1)
            pe.wait_ge(ad_in, 32)
            pe.wait_ge(ready_dve, 3)
            for half in range(KC):
                for k in range(KC):
                    i = mm(E5[:, half * B:(half + 1) * B], aw1[:, k, half * P:(half + 1) * P], cT[:, k],
                           k == 0, k == KC - 1)
            i.then_inc(setup_pe, 1)

            def l0_whole_a(m, par):
                scores(m, par)
                up_chunks(A1, sw1, par, range(4), a1_done, True)
                up_chunks(A3, sw3, par, range(4), a3_done, True)
                pe.wait_ge(l0r_in, 48)
                up_chunks(E47, rw1, par, range(4, 8), ex47_done, True)
                pe.wait_ge(sa_done, count(m, 1))
                up_chunks(A1, rw1, par, range(0, 4), ex03_done, True)

            def l0_whole_b(m, par):
                spread_gates(m, D4, (4, 5, 6, 7), cb47_done, True)
                pe.wait_ge(gs_done, count(m, 1))
                spread_gates(m, A3, (0, 1, 2, 3), cb03_done, True)
                l0_out(0, "s", (0, 1, 2, 3), start=True)
                l0_out(1, "s", (0, 1, 2, 3))
                pe.wait_ge(ge47_done, count(m, 1))
                l0_out(0, "r", (4, 5, 6, 7))
                l0_out(1, "r", (4, 5, 6, 7))
                pe.wait_ge(ge03_done, count(m, 1))
                l0_out(0, "r", (0, 1, 2, 3))
                l0_out(1, "r", (0, 1, 2, 3), done=l0_done)

            pe.wait_ge(setup_dve, 10)
            l0_whole_a((0, 0), 0)
            pe.wait_ge(peaks_dve, 5)
            mm(p_r[0:4, 0:P], peak[:], ident[:], True, True).then_inc(peaks_pe, 1)
            pe.wait_ge(peaks_dve, 7)
            mm(p_z[:, 0:4], ones4[:], peakd[:], True, True).then_inc(peaks_pe, 1)
            pe.wait_ge(scales_done, 1)
            pe.wait_ge(ad2_in, 32)
            pe.wait_ge(setup_act, 2)
            for c in range(ADAPT // 512):
                if c >= 3:
                    pe.wait_ge(wrow_dve, c - 2)
                p_ = (p_r, p_z, p_h)[c % 3]
                for k in range(KC):
                    i = mm(p_[0:B, :], ah[:, k], aw2[:, k, c * 512:(c + 1) * 512], k == 0, k == KC - 1)
                i.then_inc(adapt_pe, 1)
            l0_whole_b((0, 0), 0)
            pe.wait_ge(ready_dve, 4)
            for i_, src in enumerate((2, 1)):
                for k in range(KC):
                    i = mm(p_r[:, (i_ * KC + k) * BR:(i_ * KC + k + 1) * BR], low[:, src, k * P:(k + 1) * P],
                           ident[0:BR, 0:BR], True, True)
            i.then_inc(lowT_pe, 1)
            pe.wait_ge(ready_dve, 5)
            m0 = (0, 0)
            pe.wait_ge(l2_in, 32)
            mid_base(m0)
            low_in_rank(0, x2, u_done)
            l0_whole_a((0, 1), 1)
            mid_low(m0)
            up_base(m0)
            low_in_rank(1, g2, v_done)
            up_low(m0)
            pe.wait_ge(x3_done, 1)
            pe.wait_ge(wx_in, 16 * 3)
            project(0, 0, R, 0)
            project(0, 0, R, 1)
            project(0, 1, Z, 0)
            project(0, 1, Z, 1, projrz_done)
            pe.wait_ge(xprz_done, 1)
            project(0, 0, H, 0)
            project(0, 0, H, 1, projh_done)
            pe.wait_ge(xph_done, 1)
            l0_whole_b((0, 1), 1)
            pe.wait_ge(split_w, 6)
            blocks(pe, body)
            y_out((0, BLOCKS - 1), 1)

        @block.scalar
        def _(act):
            def func(o, i, f, **kw):
                return act.activation(o, i, f, **kw)

            def tanh_a1(m):
                act.wait_ge(a1_done, count(m, 1))
                func(sig1[:], A1[:, :], ACT.Tanh, scale=0.5).then_inc(a1_sig, 1)

            def gelu_experts(m, group, p_, ready, done):
                act.wait_ge(ready, count(m, 1))
                func(pe_e[:, group], p_[:, :], ACT.Gelu).then_inc(done, 1)

            def gelu_mid(m):
                act.wait_ge(mid_done, count(m, 1))
                func(g2[:], mid_ps, ACT.Gelu).then_inc(g2_done, 1)

            def evacuate(m, par, slot, g, ready, done=None):
                act.wait_ge(ready, count(m, 1))
                for half in range(KC):
                    i = func(xp[:, par, 0, g, half], proj_ps[:, slot, half], ACT.Identity, bias=bxh[:, g, half:half + 1],
                             scale=xscale[:, g:g + 1])
                if done is not None:
                    i.then_inc(done, 1)

            def after(m, par, s, has_y, has_l23, has_l0):
                m1, m2 = later(m, 1), later(m, 2)
                q = 1 - par
                if has_l23:
                    if s == 2:
                        gelu_mid(m1)
                    if s == 8:
                        evacuate(m1, q, 0, R, projrz_done)
                        evacuate(m1, q, 1, Z, projrz_done, xprz_done)
                    if s == 10:
                        evacuate(m1, q, 0, H, projh_done, xph_done)
                if has_l0:
                    if s == 5:
                        tanh_a1(m2)
                    if s == 9:
                        gelu_experts(m2, 1, E47, ex47_done, pe47_done)
                    if s == 11:
                        gelu_experts(m2, 0, A1, ex03_done, pe03_done)

            tanh_scale = [act.alloc_register(f"tanh_scale{g}") for g in range(3)]

            def body(m, par, has_y, has_l23, has_l0):
                for s in range(STEPS):
                    n = step_count(m, s)
                    act.wait_ge(r_done, n)
                    func(rg[:], pr, ACT.Tanh, scale=tanh_scale[R]).then_inc(rg_done, 1)
                    act.wait_ge(zsum_done, n)
                    func(zg[:], zsum[:], ACT.Tanh, scale=tanh_scale[Z]).then_inc(zg_done, 1)
                    act.wait_ge(h_done, n)
                    func(ht[:], ph, ACT.Tanh, scale=tanh_scale[H]).then_inc(ht_done, 1)
                    after(m, par, s, has_y, has_l23, has_l0)

            act.wait_ge(setup_dve, 6)
            func(l1sig[:], l1pre[:], ACT.Tanh, scale=0.5).then_inc(setup_act, 1)
            act.wait_ge(setup_pe, 5)
            for half in range(KC):
                i = func(ah[:, half], E5[:, half * B:(half + 1) * B], ACT.Gelu, bias=lnab[:, 2, half:half + 1])
            i.then_inc(setup_act, 1)
            act.wait_ge(setup_dve, 8)
            func(l1sig[:], l1pre[:], ACT.Tanh, scale=0.5).then_inc(setup_act, 1)
            m0, m1 = (0, 0), (0, 1)
            tanh_a1(m0)
            gelu_experts(m0, 1, E47, ex47_done, pe47_done)
            gelu_experts(m0, 0, A1, ex03_done, pe03_done)
            tanh_a1(m1)
            gelu_mid(m0)
            gelu_experts(m1, 1, E47, ex47_done, pe47_done)
            act.wait_ge(scales_done, 1)
            evacuate(m0, 0, 0, R, projrz_done)
            evacuate(m0, 0, 1, Z, projrz_done, xprz_done)
            evacuate(m0, 0, 0, H, projh_done, xph_done)
            gelu_experts(m1, 0, A1, ex03_done, pe03_done)
            for g in (Z, R, H):
                act.reg_load(tanh_scale[g], unscale[0:1, g:g + 1].bitcast(U32))
            blocks(act, body)

        @block.vector
        def _(dve):
            def add_router_bias(m):
                dve.wait_ge(scores_done, count(m, 1))
                dve.scalar_tensor_tensor(score[:], score_ps, -1.0, tbias[:], ALU.mult, ALU.subtract)\
                   .then_inc(score_in, 1)

            def gate_op(m, k):
                if k == 0:
                    dve.wait_ge(score_exp, count(m, 1))
                    i = dve.tensor_scalar(exp1[:], expn[:], 1.0, None, ALU.add)
                else:
                    dve.wait_ge(gating, count(m, GATE_OPS, k - GATE_OPS))
                if k in (3, 4):
                    dve.memset(holder[:], 0.0)
                if k == 1:
                    i = dve.reciprocal(sg[:], exp1[:])
                if k == 2:
                    i = dve.tensor_tensor(sel[:], sg[:], rbias[:], ALU.add)
                if k == 3:
                    i = dve.max(top8[:], sel[:])
                if k == 4:
                    i = dve.max_index(idx[:], top8[:], sel[:])
                if k == 5:
                    i = dve.tensor_copy(idxf[:], idx[:, 0:2])
                if k == 6:
                    i = dve.tensor_scalar(first[:], iota[:], idxf[:, 0:1], None, ALU.is_equal)
                if k == 7:
                    i = dve.scalar_tensor_tensor(chosen[:], iota[:], idxf[:, 1:2], first[:], ALU.is_equal, ALU.add)
                if k == 8:
                    i = dve.scalar_tensor_tensor(ssel[:], sg[:], 1.0, chosen[:], ALU.mult, ALU.mult,
                                                 accum_out=den[:, 0:1])
                if k == 9:
                    dve.tensor_scalar(den[:, 1:2], den[:, 0:1], EPS_GATE, 2.0, ALU.is_gt, ALU.mult)
                    i = dve.tensor_scalar(den[:, 2:3], den[:, 0:1], EPS_GATE, None, ALU.add)
                if k == 10:
                    dve.tensor_scalar(den[:, 3:4], den[:, 1:2], -0.5, 1.0, ALU.mult, ALU.add)
                    i = dve.reciprocal(den[:, 2:3], den[:, 2:3])
                if k == 11:
                    i = dve.tensor_scalar(scaled[:], ssel[:], den[:, 2:3], den[:, 1:2], ALU.mult, ALU.mult)
                if k == 12:
                    i = dve.scalar_tensor_tensor(comb[:], chosen[:], den[:, 3:4], scaled[:], ALU.mult, ALU.add)
                i.then_inc(gating, 1)

            def silu_a1(m):
                dve.wait_ge(a1_sig, count(m, 1))
                dve.scalar_tensor_tensor(sa[:], sig1[:], 1.0, A1[:, :], ALU.add, ALU.mult).then_inc(sa_done, 1)

            def times_a3(m):
                dve.wait_ge(a3_done, count(m, 1))
                dve.wait_ge(sa_done, count(m, 1))
                dve.tensor_tensor(gs[:], sa[:], A3[:, :], ALU.mult).then_inc(gs_done, 1)

            def times_gate(m, group, p_, ready, mine, done):
                dve.wait_ge(ready, count(m, 1))
                dve.wait_ge(mine, count(m, 1))
                dve.tensor_tensor(ge[:, group], pe_e[:, group], p_[:, :], ALU.mult).then_inc(done, 1)

            def finish_l0(m, par):
                dve.wait_ge(l0_done, count(m, 1))
                dve.scalar_tensor_tensor(x1[:], l0_ps, 1.0 / 6.0, xt[:, par], ALU.mult, ALU.add).then_inc(x1_done, 1)

            def l1(m):
                dve.wait_ge(x1_done, count(m, 1))
                g = gate2[:].unsqueeze(2).to_broadcast([P, KC, STEPS, B])
                dve.tensor_tensor(x2[:].rearrange("p k (t b) -> p k t b", b=B),
                                  x1[:].rearrange("p k (t b) -> p k t b", b=B), g, ALU.mult).then_inc(x2_done, 1)

            def keep_own(m, dst, ready, done):
                dve.wait_ge(ready, count(m, 1))
                dve.tensor_tensor(dst[:], own[:], low_ps, ALU.mult).then_inc(done, 1)

            def finish_l2(m, par):
                dve.wait_ge(l2_done, count(m, 1))
                dve.scalar_tensor_tensor(x3[:, par], x2[:], 2.0, mid_ps, ALU.mult, ALU.add).then_inc(x3_done, 1)

            def split(par, part, gates, waits, done):
                for q, v in waits:
                    dve.wait_ge(q, v)
                a_, b_ = gates
                hi = xpv[:, par, part - 1, a_:b_].rearrange("p g k (t two) -> p (g k) t two", two=2)[:, :, :, 1]
                src = xp[:, par, part - 1, a_:b_].rearrange("p g k t -> p (g k) t")
                dst = xp[:, par, part, a_:b_].rearrange("p g k t -> p (g k) t")
                dve.tensor_tensor(dst, src, hi, ALU.subtract).then_inc(done, 1)

            def y_add(m, par):
                dve.wait_ge(y_done, count(m, 1))
                if not (type(m[0]) is int and m[1] == 0):
                    dve.wait_ge(stored, count(m, 16, -16))
                for half in range(KC):
                    i = dve.scalar_tensor_tensor(osb[:, half], y_ps[:, half], bq[:, half:half + 1], x3[:, par, half],
                                                 ALU.add, ALU.add)
                i.then_inc(out_done, 1)

            def early(m, par, s, has_y, has_l23, has_l0):
                m1, m2 = later(m, 1), later(m, 2)
                q = 1 - par
                if has_l23:
                    if s == 0:
                        finish_l0(m1, q)
                    if s == 2:
                        keep_own(m1, um, u_done, um_done)
                    if s == 5:
                        keep_own(m1, vm, v_done, vm_done)
                    if s == 6:
                        finish_l2(m1, q)
                    if s == 9:
                        split(q, 1, (Z, H), [(xprz_done, count(m1, 1))], rz_mid)
                    if s == 11:
                        split(q, 2, (Z, H), [(rz_mid, count(m1, 1))], rz_low)
                if has_y and s == 2:
                    y_add(later(m, -1), q)
                if has_l0:
                    if s == 1:
                        add_router_bias(m2)
                    if s == 4:
                        gate_op(m2, 0)
                    if s == 6:
                        silu_a1(m2)
                    if s == 5:
                        gate_op(m2, 2)
                    if s == 7:
                        gate_op(m2, 6)
                    if s == 8:
                        times_a3(m2)
                    if s == 10:
                        gate_op(m2, 11)
                    if s == 12:
                        times_gate(m2, 1, D4, cb47_done, pe47_done, ge47_done)
                    if s == 14:
                        times_gate(m2, 0, A3, cb03_done, pe03_done, ge03_done)

            def late(m, par, s, has_y, has_l23, has_l0):
                m1, m2 = later(m, 1), later(m, 2)
                q = 1 - par
                if has_l23:
                    if s == 0:
                        l1(m1)
                    if s == 13:
                        split(q, 1, (H, H + 1), [(xph_done, count(m1, 1))], h_mid_x)
                    if s == 14:
                        split(q, 2, (H, H + 1), [(h_mid_x, count(m1, 1))], h_low_x)
                if has_l0:
                    for at, k in ((4, 1), (5, 3), (6, 4), (6, 5), (7, 7), (8, 8), (9, 9), (9, 10), (10, 12)):
                        if s == at:
                            gate_op(m2, k)

            def body(m, par, has_y, has_l23, has_l0):
                for s in range(STEPS):
                    n = step_count(m, s)
                    bp, bs = before(par, s)
                    old = hist[:, bp, :, bs * B:(bs + 1) * B]
                    new = hist[:, par, :, s * B:(s + 1) * B]
                    early(m, par, s, has_y, has_l23, has_l0)
                    dve.wait_ge(rg_done, n)
                    dve.scalar_tensor_tensor(rhp[:, :, 0], rg[:], 1.0, old, ALU.add, ALU.mult).then_inc(rh_hi, 1)
                    dve.scalar_tensor_tensor(rh[:], rg[:], 1.0, old, ALU.add, ALU.mult).then_inc(rh_all, 1)
                    dve.wait_ge(z_done, n)
                    dve.tensor_reduce(zsum[:], pz.rearrange("p k a c -> p k c a"), AX_X, ALU.add).then_inc(zsum_done, 1)
                    dve.wait_ge(rh_all, n)
                    dve.tensor_tensor(rhp[:, :, 1], rh[:], rhp[:, :, 0], ALU.subtract).then_inc(rh_low, 1)
                    late(m, par, s, has_y, has_l23, has_l0)
                    dve.wait_ge(zg_done, n)
                    dve.tensor_scalar(zm[:], zg[:], -1.0, sscale[:], ALU.add, ALU.mult).then_inc(zm_done, 1)
                    dve.wait_ge(zm_done, n)
                    dve.scalar_tensor_tensor(zh[:], zg[:], 1.0, old, ALU.add, ALU.mult)
                    dve.wait_ge(ht_done, n)
                    dve.tensor_tensor(fresh[:], zm[:], ht[:], ALU.mult).then_inc(fresh_done, 1)
                    dve.wait_ge(fresh_done, n)
                    dve.scalar_tensor_tensor(state[:, :, 0], zh[:], 0.5, fresh[:], ALU.mult, ALU.subtract)\
                       .then_inc(st_hi, 1)
                    dve.scalar_tensor_tensor(new, zh[:], 0.5, fresh[:], ALU.mult, ALU.subtract).then_inc(st_all, 1)
                    dve.wait_ge(st_all, n + 1)
                    dve.tensor_tensor(state[:, :, 1], new, state[:, :, 0], ALU.subtract).then_inc(st_low, 1)

            c_ = [0]

            def link(i):
                c_[0] += 1
                i.then_inc(setup_dve, 1)
                dve.wait_ge(setup_dve, c_[0])

            dve.wait_ge(cond_in, 32)
            link(dve.bn_stats(stats[:], cond[:]))
            link(dve.bn_aggr(meanvar[:], stats[:]))
            dve.memset(lnv[:, 1:2], -0.5)
            link(dve.tensor_scalar(lnv[:, 0:1], meanvar[:, 1:2], EPS_LN, None, ALU.add))
            dve.wait_ge(setup_pool, 1)
            dve.tensor_scalar(cn[:], cond[:], meanvar[:, 0:1], lnv[:, 2:3], ALU.subtract, ALU.mult).then_inc(ready_dve, 1)
            dve.wait_ge(setup_pe, 1)
            link(dve.tensor_copy(tbias[:], A1[:, 0:EXPERTS]))
            dve.wait_ge(setup_pe, 2)
            dve.wait_ge(l1_in, 48)
            for half in range(KC):
                link(dve.tensor_scalar(l1pre[:, half], A3[:, half * B:(half + 1) * B], l1b[:, 0, half:half + 1], None,
                                       ALU.add))
            dve.wait_ge(setup_act, 1)
            dve.scalar_tensor_tensor(l1h[:], l1sig[:], 1.0, l1pre[:], ALU.add, ALU.mult).then_inc(ready_dve, 1)
            dve.wait_ge(setup_pe, 3)
            dve.wait_ge(ad_in, 32)
            for k in range(KC):
                i = dve.tensor_scalar(cT[:, k], E47[:, k * B:(k + 1) * B], lnab[:, 0, k:k + 1], lnab[:, 1, k:k + 1],
                                      ALU.mult, ALU.add)
            i.then_inc(ready_dve, 1)
            dve.wait_ge(setup_pe, 4)
            for half in range(KC):
                link(dve.tensor_scalar(l1pre[:, half], D4[:, half * B:(half + 1) * B], 0.5, l1b[:, 1, half:half + 1],
                                       ALU.mult, ALU.add))
            dve.wait_ge(setup_act, 3)
            link(dve.tensor_scalar(gate2[:], l1sig[:], 0.5, 2.5, ALU.mult, ALU.add))
            dve.wait_ge(bias_in, 16 * 3)
            dve.tensor_copy(identb[:], ident[:])
            link(dve.tensor_tensor(bxh[:], bx[:], bh[:], ALU.add))

            def find_scales():
                dve.memset(ones4[:], 1.0)
                dve.wait_ge(rec_in, 48)
                for g in range(3):
                    dve.tensor_reduce(peak[:, g:g + 1], wh[:, g], AX_XY, ALU.max, apply_absolute_value=True)\
                       .then_inc(peaks_dve, 1)
                dve.tensor_reduce(peak[:, 3:4], condT, AX_XY, ALU.max, apply_absolute_value=True).then_inc(peaks_dve, 1)
                dve.wait_ge(peaks_dve, 4)
                dve.tensor_scalar(peak[:, 3:4], peak[:, 3:4], 1.0, None, ALU.max).then_inc(peaks_dve, 1)
                dve.wait_ge(peaks_pe, 1)
                dve.tensor_reduce(peak4[:], p_r[0:4, 0:P], AX_X, ALU.max).then_inc(peaks_dve, 1)
                dve.wait_ge(peaks_dve, 6)
                dve.tensor_scalar(peakd[:], ident[0:4, 0:4], peak4[:], None, ALU.mult).then_inc(peaks_dve, 1)
                dve.wait_ge(peaks_pe, 2)
                dve.tensor_scalar(inv[:], p_z[:, 0:4], LEAST_PEAK, None, ALU.max).then_inc(peaks_dve, 1)
                dve.wait_ge(peaks_dve, 8)
                dve.tensor_scalar(power[:].bitcast(U32), inv[:].bitcast(U32), EXPONENT_BITS, None, ALU.bitwise_and)\
                   .then_inc(peaks_dve, 1)
                dve.wait_ge(peaks_dve, 9)
                dve.reciprocal(inv[:], power[:]).then_inc(peaks_dve, 1)
                dve.wait_ge(peaks_dve, 10)
                dve.tensor_scalar(wscale[:], inv[:, 0:3], 2.0 ** W_TOP, None, ALU.mult)
                dve.tensor_scalar(sscale[:], inv[:, 3:4], 2.0 ** S_TOP, None, ALU.mult)
                dve.tensor_scalar(qscale[:], power[:, 3:4], 0.5 * 2.0 ** -S_TOP, None, ALU.mult)
                for g, times, half in ((Z, 2.0, 0.5), (R, 2.0, 0.5), (H, 4.0, 1.0)):
                    top = 2.0 ** (W_TOP + S_TOP) * times
                    dve.tensor_scalar(xscale[:, g:g + 1], inv[:, g:g + 1], inv[:, 3:4], top, ALU.mult, ALU.mult)
                    i = dve.tensor_scalar(unscale[:, g:g + 1], power[:, g:g + 1], power[:, 3:4], half / top,
                                          ALU.mult, ALU.mult)
                i.then_inc(peaks_dve, 1)
                dve.wait_ge(peaks_dve, 11)
                for g in range(3):
                    i = dve.tensor_scalar(bxh[:, g], bxh[:, g], xscale[:, g:g + 1], None, ALU.mult)
                i.then_inc(scales_done, 1)

            def gates_whole(m):
                for k in range(GATE_OPS):
                    gate_op(m, k)

            def l0_whole_a(m):
                add_router_bias(m)
                gates_whole(m)
                silu_a1(m)
                times_a3(m)

            def l0_whole_b(m):
                times_gate(m, 1, D4, cb47_done, pe47_done, ge47_done)
                times_gate(m, 0, A3, cb03_done, pe03_done, ge03_done)

            m0, m1 = (0, 0), (0, 1)
            dve.wait_ge(const_in, 64)
            l0_whole_a(m0)
            find_scales()
            for c in range(ADAPT // 512):
                dve.wait_ge(adapt_pe, c + 1)
                dve.tensor_copy(wrow[:, c * 512:(c + 1) * 512], (p_r, p_z, p_h)[c % 3][0:B, :]).then_inc(wrow_dve, 1)
            dve.tensor_scalar(sscale2[:], sscale[:], 2.0, None, ALU.mult).then_inc(peaks_dve, 1)
            dve.wait_ge(peaks_dve, 12)
            last = hist[:, 1, :, (STEPS - 1) * B:STEPS * B]
            dve.tensor_scalar(state[:, :, 0], condT, sscale2[:], None, ALU.mult).then_inc(st_hi, 1)
            dve.tensor_scalar(last, condT, sscale2[:], None, ALU.mult).then_inc(st_all, 1)
            dve.wait_ge(st_all, 1)
            dve.tensor_tensor(state[:, :, 1], last, state[:, :, 0], ALU.subtract).then_inc(st_low, 1)
            l0_whole_b(m0)
            finish_l0(m0, 0)
            l1(m0)
            dve.wait_ge(low_in, 4 * B * 16)
            dve.wait_ge(abias_in, 16 * B)
            dve.tensor_tensor(low[:], low[:], abias[:], ALU.add).then_inc(ready_dve, 1)
            dve.wait_ge(lowT_pe, 1)
            dve.tensor_copy(a2b1[:], p_r[:, 0:2 * KC * BR].rearrange("p (i k c) -> p i k c", i=2, k=KC))\
               .then_inc(ready_dve, 1)
            keep_own(m0, um, u_done, um_done)
            l0_whole_a(m1)
            keep_own(m0, vm, v_done, vm_done)
            finish_l2(m0, 0)
            split(0, 1, (Z, H), [(xprz_done, 1)], rz_mid)
            split(0, 2, (Z, H), [(rz_mid, 1)], rz_low)
            split(0, 1, (H, H + 1), [(xph_done, 1)], h_mid_x)
            split(0, 2, (H, H + 1), [(h_mid_x, 1)], h_low_x)
            l0_whole_b(m1)
            blocks(dve, body)
            y_add((0, BLOCKS - 1), 1)


def kernel(**inputs):
    import concourse.bacc as _bacc
    from concourse.bass_utils import run_bass_kernel_spmd as _run

    f = {k: np.asarray(v) for k, v in inputs.items()}

    def rows(w):
        return np.ascontiguousarray(w.reshape(-1, P, w.shape[-1]).transpose(1, 0, 2))

    def vec(v):
        return v.reshape(KC, P).T

    g3 = ("z", "r", "h")
    L0, L1, L2, L3 = ("L0_cond_", "L1_cond_", "L2_cond_", "L3_cond_")
    w2 = f[L2 + "W2"].reshape(D, 4, D, RANK).transpose(0, 1, 3, 2).reshape(D, ADAPT)
    tok = np.arange(TOK)
    arrays = {
        "xT": rows(f["x"].transpose(2, 1, 0).reshape(D, T * B)),
        "cond_tok": rows(f["cond_1024"].T[:, tok % B]),
        "cond": f["cond_1024"],
        "sw1": rows(f[L0 + "sw1"].T), "sw3": rows(f[L0 + "sw3"].T), "sw2": rows(f[L0 + "sw2"].T),
        "rw1": rows(f[L0 + "rw1"].reshape(EXPERTS * HR, D).T),
        "rw2": rows(f[L0 + "rw2"].transpose(0, 2, 1).reshape(EXPERTS * HR, D)),
        "rw": rows(f[L0 + "router_w"].T), "rtw": rows(f[L0 + "router_t_w"].T), "rbias": f[L0 + "router_bias"],
        "l1w1": rows(f[L1 + "W1"].T), "l1w2": rows(f[L1 + "W2"].T),
        "l1b": np.stack([vec(f[L1 + "b1"]), vec(f[L1 + "b2"])], 1),
        "down": rows(f[L2 + "base_down"]), "up": rows(f[L2 + "base_up"].T),
        "aw1": rows(f[L2 + "W1"]), "aw2": rows(w2),
        "lnab": np.stack([vec(f[L2 + n]) for n in ("ln_gamma", "ln_beta", "bias1")], 1),
        "abias": f[L2 + "bias2"].reshape(4, D, RANK).transpose(2, 0, 1),
        "wx": np.stack([rows(f[L3 + "Wx" + g].T) for g in g3]),
        "wh": np.stack([rows(f[L3 + "Wh" + g].T) for g in g3]),
        "wq": rows(f[L3 + "Whq"].T),
        "bx": np.stack([vec(f[L3 + "bx" + g]) for g in g3], 1),
        "bh": np.stack([vec(f[L3 + "bh" + g]) for g in g3], 1),
        "bq": vec(f[L3 + "bhq"]),
        "ident": np.eye(P, dtype=np.float32),
        "iota": np.tile(np.arange(EXPERTS, dtype=np.float32), (P, 1)),
        "own": (np.arange(BR)[:, None] // RANK == tok[None] % B).astype(np.float32),
    }
    nc = _bacc.Bacc("TRN2", target_bir_lowering=False, num_devices=1)
    feeds, handles = {}, {}
    for name, v in arrays.items():
        v = np.ascontiguousarray(v)
        feeds[f"in_{name}"] = v
        handles[name] = nc.dram_tensor(f"in_{name}", v.shape, mybir.dt.from_np(v.dtype), kind="ExternalInput").ap()
    out = nc.dram_tensor("out_0", (P, KC, T * B), F32, kind="ExternalOutput").ap()
    build(nc, handles, out)
    r = _run(nc, [feeds], core_ids=[0])
    got = r.results[0]["out_0"]
    return np.ascontiguousarray(got.reshape(P, KC, T, B).transpose(3, 2, 1, 0).reshape(B, T, D))
```

```python
from contextlib import ExitStack

import numpy as np
import concourse.bass as bass
from concourse import mybir

ALU = mybir.AluOpType
ACT = mybir.ActivationFunctionType
F32 = mybir.dt.float32
BF16 = mybir.dt.bfloat16
F16 = mybir.dt.float16
U32 = mybir.dt.uint32
AX_X = mybir.AxisListType.X
AX_XY = mybir.AxisListType.XY

P = 128
B, T, D = 8, 512, 256
KC = D // P
TOK = P
STEPS = TOK // B
BLOCKS = T // STEPS
HS = 512
EXPERTS, HR = 8, 128
RANK = 8
BR = B * RANK
ADAPT = 4 * RANK * D
XPARTS = 3
HPARTS = 2
W_TOP, S_TOP = 14, 12
GATE_OPS = 13
Z, R, H = range(3)
LOW_ORDER = (2, 1, 3, 0)
EPS_GATE, EPS_LN = 1e-9, 1e-5
LEAST_PEAK = 2.0 ** -40
EXPONENT_BITS = 0x7F800000


def count(m, per, extra=0):
    return m[0] * (2 * per) + ((m[1] + 1) * per + extra)


def pair_count(m, per):
    return m[0] * per + (m[1] // 2 + 1) * per


def step_count(m, s):
    return m[0] * (2 * STEPS) + (m[1] * STEPS + s + 1)


def token_start(m):
    return m[0] * (2 * TOK) + m[1] * TOK


def build(nc, a, out):
    with ExitStack() as ctx:
        def sb(name, shape, dt=F32):
            return ctx.enter_context(nc.sbuf_tensor(name, shape, dt))

        def ps(name, shape=(P, 512), dt=F32):
            return ctx.enter_context(nc.psum_tensor(name, list(shape), dt))

        def sem(name):
            return ctx.enter_context(nc.semaphore(name))

        sw1 = sb("sw1", [P, KC, HS])
        sw3 = sb("sw3", [P, KC, HS])
        sw2 = sb("sw2", [P, HS // P, D])
        rw1 = sb("rw1", [P, KC, EXPERTS * HR])
        rw2 = sb("rw2", [P, EXPERTS, D])
        rw = sb("rw", [P, KC, EXPERTS])
        rtw = sb("rtw", [P, KC, EXPERTS])
        rbias = sb("rbias", [P, EXPERTS])
        l1w1 = sb("l1w1", [P, KC, D])
        l1w2 = sb("l1w2", [P, KC, D])
        l1b = sb("l1b", [P, 2, KC])
        down = sb("down", [P, KC, D])
        up = sb("up", [P, KC, D])
        aw1 = sb("aw1", [P, KC, D])
        aw2 = sb("aw2", [P, KC, ADAPT])
        lnab = sb("lnab", [P, 3, KC])
        abias = sb("abias", [BR, 4, D])
        wx = sb("wx", [P, 3, KC, D])
        wh = sb("wh", [P, 3, KC, D])
        wrest = sb("wrest", [P, 3, KC, D])
        whp = sb("whp", [P, HPARTS, 3, KC, D], F16)
        wq = sb("wq", [P, KC, D])
        wqh = sb("wqh", [P, KC, D])
        brow = sb("brow", [XPARTS, 3, D], BF16)
        ones_row = sb("ones_row", [XPARTS, TOK], BF16)
        bq = sb("bq", [P, KC])
        ident = sb("ident", [P, P])
        iota = sb("iota", [P, EXPERTS])
        own = sb("own", [BR, TOK])
        cond_tok = sb("cond_tok", [P, KC, TOK])
        condT = cond_tok[:, :, 0:B]
        cond = sb("cond", [B, D])

        tbias = sb("tbias", [P, EXPERTS])
        l1pre = sb("l1pre", [P, KC, B])
        l1sig = sb("l1sig", [P, KC, B])
        l1h = sb("l1h", [P, KC, B])
        gate2 = sb("gate2", [P, KC, B])
        stats = sb("stats", [B, 6])
        meanvar = sb("meanvar", [B, 2])
        lnv = sb("lnv", [B, 3])
        cn = sb("cn", [B, D])
        cT = sb("cT", [P, KC, B])
        ah = sb("ah", [P, KC, B])
        wrow = sb("wrow", [B, 2, RANK * D])
        low = sb("low", [BR, 4, D])
        a2b1 = sb("a2b1", [P, 2, KC, BR])

        xt = sb("xt", [P, 2, KC, TOK])
        holder = sb("holder", [P, 1])
        score = sb("score", [P, EXPERTS])
        euler = sb("euler", [P, EXPERTS])
        expn = sb("expn", [P, EXPERTS])
        exp1 = sb("exp1", [P, EXPERTS])
        sg = sb("sg", [P, EXPERTS])
        sel = sb("sel", [P, EXPERTS])
        top8 = sb("top8", [P, 8])
        idx = sb("idx", [P, 8], U32)
        idxf = sb("idxf", [P, 2])
        first = sb("first", [P, EXPERTS])
        chosen = sb("chosen", [P, EXPERTS])
        ssel = sb("ssel", [P, EXPERTS])
        den = sb("den", [P, 4])
        scaled = sb("scaled", [P, EXPERTS])
        comb = sb("comb", [P, EXPERTS])
        sig1 = sb("sig1", [P, HS])
        sa = sb("sa", [P, HS])
        gs = sb("gs", [P, HS])
        pe_e = sb("pe_e", [P, 2, 4 * TOK])
        ge = sb("ge", [P, 2, 4 * TOK])
        x1 = sb("x1", [P, KC, TOK])
        x2 = sb("x2", [P, KC, TOK])
        g2 = sb("g2", [P, KC, TOK])
        um = sb("um", [BR, TOK])
        vm = sb("vm", [BR, TOK])
        x3 = sb("x3", [P, 2, KC, TOK])
        bx = sb("bx", [XPARTS, 3, D])
        bh = sb("bh", [XPARTS, 3, D])
        bpart = sb("bpart", [XPARTS, 2, 3, D], BF16)
        hist = sb("hist", [P, 2, KC, TOK])
        state = sb("state", [P, KC, HPARTS, B], F16)
        rh = sb("rh", [P, KC, B])
        rhp = sb("rhp", [P, KC, HPARTS, B], F16)
        peak = sb("peak", [P, 4])
        peak4 = sb("peak4", [4, 1])
        peakd = sb("peakd", [4, 4])
        ones4 = sb("ones4", [4, P])
        power = sb("power", [P, 4])
        inv = sb("inv", [P, 4])
        wscale = sb("wscale", [P, 3])
        sscale = sb("sscale", [P, 1])
        xscale = sb("xscale", [P, 3])
        unscale = sb("unscale", [P, 3])
        qscale = sb("qscale", [P, 1])
        sscale2 = sb("sscale2", [P, 1])
        zm = sb("zm", [P, KC, B])
        rg = sb("rg", [P, KC, B])
        zg = sb("zg", [P, KC, B])
        zsum = sb("zsum", [P, KC, B])
        zh = sb("zh", [P, KC, B])
        ht = sb("ht", [P, KC, B])
        fresh = sb("fresh", [P, KC, B])
        osb = sb("osb", [P, KC, TOK])

        def before(par, s):
            return (par, s - 1) if s else (1 - par, STEPS - 1)

        gate_rh = [ps(f"gate_rh{i}") for i in range(2)]
        gate_z = [ps(f"gate_z{i}") for i in range(2)]
        rh_ps = [t[:, :].rearrange("p (g k t) -> p g k t", g=2, k=KC) for t in gate_rh]
        z_ps = [t[:, :].rearrange("p (a k t) -> p a k t", a=HPARTS, k=KC) for t in gate_z]
        spare = (gate_rh[0], gate_z[0], gate_rh[1])
        A1, A3, E47, E5 = (ps(f"bank{i}") for i in range(4))
        y_ps = E47[:, 0:KC * TOK].rearrange("p (k t) -> p k t", k=KC)
        score_ps = E47[:, KC * TOK:KC * TOK + EXPERTS]
        l0_ps = E5[:, 0:KC * TOK].rearrange("p (k t) -> p k t", k=KC)
        mid_ps = E5[:, 0:KC * TOK].rearrange("p (k t) -> p k t", k=KC)
        low_ps = E5[0:BR, KC * TOK:(KC + 1) * TOK]

        cond_in, l1_in, ad_in, l0_in, l0w_in, l0r_in, l2_in, rec_in, const_in, wx_in = (
            sem(n) for n in ("cond_in", "l1_in", "ad_in", "l0_in", "l0w_in", "l0r_in", "l2_in", "rec_in",
                             "const_in", "wx_in"))
        bq_in, ident_in, l1w2_in, abias_in, bias_in, wq_in, wx_scaled, setup_pool, peaks_dve, peaks_pe, scales_done = (
            sem(n) for n in ("bq_in", "ident_in", "l1w2_in", "abias_in", "bias_in", "wq_in", "wx_scaled", "setup_pool", "peaks_dve", "peaks_pe", "scales_done"))
        x_in = [sem("x_in0"), sem("x_in1")]
        stored = sem("stored")
        ad2_in = [sem(f"ad2_in{i}") for i in range(4)]
        low_in = [sem(f"low_in{i}") for i in range(4)]
        split_w, setup_pe, setup_act, setup_dve, wrow_dve, adapt_pe, lowT_pe, ready_dve = (
            sem(n) for n in ("split_w", "setup_pe", "setup_act", "setup_dve", "wrow_dve", "adapt_pe", "lowT_pe",
                             "ready_dve"))
        names = ("scores_done", "a1_done", "a3_done", "ex47_done", "ex03_done", "cb47_done", "cb03_done", "l0_done",
                 "u_done", "mid_done", "v_done", "l2_done", "y_done",
                 "score_exp", "a1_sig", "score_in", "gating", "sa_done", "gs_done", "pe47_done", "ge47_done", "pe03_done", "ge03_done",
                 "x1_done", "x2_done", "um_done", "g2_done", "vm_done", "x3_done", "out_done")
        (scores_done, a1_done, a3_done, ex47_done, ex03_done, cb47_done, cb03_done, l0_done,
         u_done, mid_done, v_done, l2_done, y_done,
         score_exp, a1_sig, score_in, gating, sa_done, gs_done, pe47_done, ge47_done, pe03_done, ge03_done,
         x1_done, x2_done, um_done, g2_done, vm_done, x3_done, out_done) = (sem(n) for n in names)
        (r_done, z_done, h_done, rg_done, zg_done, ht_done, rh_hi, rh_all, rh_low, zsum_done, zm_done,
         fresh_done, st_hi, st_all, st_low) = (
            sem(n) for n in ("r_done", "z_done", "h_done", "rg_done", "zg_done", "ht_done", "rh_hi", "rh_all",
                             "rh_low", "zsum_done", "zm_done", "fresh_done", "st_hi", "st_all", "st_low"))

        block = ctx.enter_context(nc.Block())

        def blocks(eng, body):
            body((0, 0), 0, False, True, True)
            with eng.Fori(0, (BLOCKS - 4) // 2) as j:
                body((j, 1), 1, True, True, True)
                body((j, 2), 0, True, True, True)
            body((0, BLOCKS - 3), 1, True, True, True)
            body((0, BLOCKS - 2), 0, True, True, False)
            body((0, BLOCKS - 1), 1, True, False, False)

        def later(m, d):
            return (m[0], m[1] + d)

        @block.sync
        def _(sp):
            sp.dma_start(cond_tok[:], a["cond_tok"]).then_inc(cond_in, 16)
            sp.dma_start(cond[:], a["cond"]).then_inc(cond_in, 16)
            sp.dma_start(rtw[:], a["rtw"]).then_inc(l0_in, 16)
            sp.dma_start(rw[:], a["rw"]).then_inc(l0_in, 16)
            sp.dma_start(lnab[:], a["lnab"]).then_inc(ad_in, 16)
            sp.dma_start(aw1[:], a["aw1"]).then_inc(ad_in, 16)
            sp.dma_start(sw1[:], a["sw1"]).then_inc(l0w_in, 16)
            sp.dma_start(sw3[:], a["sw3"]).then_inc(l0w_in, 16)
            sp.dma_start(rw1[:], a["rw1"]).then_inc(l0r_in, 16)
            sp.dma_start(sw2[:], a["sw2"]).then_inc(l0r_in, 16)
            sp.dma_start(rw2[:], a["rw2"]).then_inc(l0r_in, 16)
            sp.dma_start(iota[:], a["iota"]).then_inc(const_in, 16)
            sp.dma_start(rbias[:], a["rbias"].partition_broadcast(P)).then_inc(const_in, 16)
            sp.dma_start(own[:], a["own"]).then_inc(const_in, 16)
            for g in range(3):
                sp.dma_start(wh[:, g], a["wh"][g]).then_inc(rec_in, 16)
            sp.dma_start(bx[:], a["bx"].partition_broadcast(XPARTS)).then_inc(bias_in, 16)
            sp.dma_start(bh[:], a["bh"].partition_broadcast(XPARTS)).then_inc(bias_in, 16)
            for i in LOW_ORDER:
                columns = slice(i * RANK * D, (i + 1) * RANK * D)
                sp.dma_start(aw2[:, :, columns], a["aw2"][:, :, columns]).then_inc(ad2_in[i], 16)
            for b in range(B):
                sp.dma_start(abias[b * RANK:(b + 1) * RANK], a["abias"]).then_inc(abias_in, 16)
            sp.dma_start(down[:], a["down"]).then_inc(l2_in, 16)
            sp.dma_start(up[:], a["up"]).then_inc(l2_in, 16)
            for g in range(3):
                sp.dma_start(wx[:, g], a["wx"][g]).then_inc(wx_in, 16)
            sp.dma_start(wq[:], a["wq"]).then_inc(wq_in, 16)
            sp.dma_start(bq[:], a["bq"]).then_inc(bq_in, 16)
            for at, i in enumerate(LOW_ORDER):
                sp.wait_ge(wrow_dve, 4 * (at + 1))
                for b in range(B):
                    src = wrow[b:b + 1, at % 2].rearrange("b (r d) -> b r d", r=RANK)
                    sp.dma_start(low[b * RANK:(b + 1) * RANK, i, :], src).then_inc(low_in[i], 16)

        @block.gpsimd
        def _(pool):
            pool.dma_start(ident[:], a["ident"]).then_inc(ident_in, 16)
            pool.dma_start(l1w1[:], a["l1w1"]).then_inc(l1_in, 16)
            pool.dma_start(l1b[:], a["l1b"]).then_inc(l1_in, 16)
            pool.dma_start(l1w2[:], a["l1w2"]).then_inc(l1w2_in, 16)
            pool.wait_ge(setup_dve, 3)
            pool.tensor_tensor(lnv[:, 2:3], lnv[:, 0:1], lnv[:, 1:2], ALU.pow).then_inc(setup_pool, 1)
            pool.dma_start(xt[:, 0], a["xT"][:, :, 0:TOK]).then_inc(x_in[0], 16)
            pool.dma_start(xt[:, 1], a["xT"][:, :, TOK:2 * TOK]).then_inc(x_in[1], 16)

            def exp_scores(m):
                pool.wait_ge(score_in, count(m, 1))
                pool.tensor_tensor(expn[:], euler[:], score[:], ALU.pow).then_inc(score_exp, 1)

            pool.memset(euler[:], float(np.e)).then_inc(setup_pool, 1)
            pool.wait_ge(setup_pool, 2)
            exp_scores((0, 0))
            pool.wait_ge(scales_done, 1)
            for g in range(3):
                pool.tensor_scalar(wrest[:, g], wh[:, g], wscale[:, g:g + 1], None, ALU.mult).then_inc(split_w, 1)
            pool.wait_ge(split_w, 3)
            pool.tensor_copy(whp[:, 0], wrest[:]).then_inc(split_w, 1)
            pool.wait_ge(split_w, 4)
            pool.tensor_tensor(whp[:, 1], wrest[:], whp[:, 0], ALU.subtract).then_inc(split_w, 1)
            pool.wait_ge(wq_in, 16)
            pool.tensor_scalar(wqh[:], wq[:], qscale[:], None, ALU.mult).then_inc(split_w, 1)

            def xcols(m):
                at = token_start(m)
                return at if type(at) is int else pool.snap(at)

            def load_x(at, par):
                pool.dma_start(xt[:, par], a["xT"][:, :, bass.ds(at, TOK)]).then_inc(x_in[par], 16)

            def store(m):
                at = xcols(m)
                pool.wait_ge(out_done, count(m, 1))
                pool.dma_start(out[:, :, bass.ds(at, TOK)], osb[:]).then_inc(stored, 16)

            pool.wait_ge(wx_in, 16 * 3)
            for g in range(3):
                pool.tensor_scalar(wx[:, g], wx[:, g], xscale[:, g:g + 1], None, ALU.mult).then_inc(wx_scaled, 1)

            pool.wait_ge(x1_done, 1)
            load_x(2 * TOK, 0)
            exp_scores((0, 1))

            def body(m, par, has_y, has_l23, has_l0):
                if has_l0 and not (type(m[0]) is int and m[1] + 3 >= BLOCKS):
                    x_block = xcols(later(m, 3))
                    pool.wait_ge(x1_done, count(later(m, 1), 1))
                    load_x(x_block, 1 - par)
                if has_l0:
                    exp_scores(later(m, 2))
                if has_y:
                    store(later(m, -1))

            blocks(pool, body)
            store((0, BLOCKS - 1))
            pool.wait_ge(stored, 16 * BLOCKS)


        @block.tensor
        def _(pe):
            def mm(o, w, x, start, stop):
                return pe.matmul(o, w, x, start=start, stop=stop, skip_group_check=True)

            def scores(m, par):
                pe.wait_ge(x_in[par], pair_count(m, 16))
                for k in range(KC):
                    i = mm(score_ps, xt[:, par, k], rw[:, k], k == 0, k == KC - 1)
                i.then_inc(scores_done, 1)

            def up_chunks(ps_, w, par, chunks, done, last):
                for c in chunks:
                    for k in range(KC):
                        i = mm(ps_[:, c % 4 * TOK:(c % 4 + 1) * TOK], w[:, k, c * P:(c + 1) * P], xt[:, par, k],
                               k == 0, k == KC - 1)
                if last:
                    i.then_inc(done, 1)

            def spread_gates(m, ps_, experts, done, last):
                pe.wait_ge(gating, count(m, GATE_OPS))
                for e in experts:
                    i = mm(ps_[:, e % 4 * TOK:(e % 4 + 1) * TOK], comb[:, e:e + 1].to_broadcast([P, P]), ident[:],
                           True, True)
                if last:
                    i.then_inc(done, 1)

            def l0_out(half, kind, chunks, start=False, done=None):
                for c in chunks:
                    w = sw2 if kind == "s" else rw2
                    g = gs[:, c * TOK:(c + 1) * TOK] if kind == "s" else ge[:, c // 4, c % 4 * TOK:(c % 4 + 1) * TOK]
                    i = mm(l0_ps[:, half], w[:, c, half * P:(half + 1) * P], g, start and c == chunks[0], False)
                if done is not None:
                    i.then_inc(done, 1)

            def mid_base(m):
                pe.wait_ge(x2_done, count(m, 1))
                for half in range(KC):
                    for k in range(KC):
                        mm(mid_ps[:, half], down[:, k, half * P:(half + 1) * P], x2[:, k],
                           half == 0 and k == 0, False)

            def low_in_rank(w, x, done):
                for k in range(KC):
                    i = mm(low_ps, a2b1[:, w, k], x[:, k], False, k == KC - 1)
                i.then_inc(done, 1)

            def mid_low(m):
                pe.wait_ge(um_done, count(m, 1))
                for half in range(KC):
                    i = mm(mid_ps[:, half], low[:, 3, half * P:(half + 1) * P], um[:], False, True)
                i.then_inc(mid_done, 1)

            def up_base(m):
                pe.wait_ge(g2_done, count(m, 1))
                for half in range(KC):
                    for k in range(KC):
                        mm(mid_ps[:, half], up[:, k, half * P:(half + 1) * P], g2[:, k], half == 0 and k == 0, False)

            def up_low(m):
                pe.wait_ge(vm_done, count(m, 1))
                for half in range(KC):
                    i = mm(mid_ps[:, half], low[:, 0, half * P:(half + 1) * P], vm[:], False, True)
                i.then_inc(l2_done, 1)

            def project(par, g, half):
                o = z_ps[par][:, 0, half] if g == Z else rh_ps[par][:, g - 1, half]
                mm(o, brow[:, g, half * P:(half + 1) * P], ones_row[:], g != H and half == 0, False)
                for k in range(KC):
                    mm(o, wx[:, g, k, half * P:(half + 1) * P], x3[:, par, k], False, False)

            def y_out(m, par):
                pe.wait_ge(st_all, step_count(m, STEPS - 1) + 1)
                for half in range(KC):
                    for k in range(KC):
                        i = mm(y_ps[:, half], wqh[:, k, half * P:(half + 1) * P], hist[:, par, k], k == 0, k == KC - 1)
                i.then_inc(y_done, 1)

            def recur(p_, g, wpart, view, part, last=None):
                for half in range(KC):
                    for k in range(KC):
                        i = mm(p_[:, half], whp[:, wpart, g, k, half * P:(half + 1) * P], view[:, k, part], False,
                               last is not None)
                if last is not None:
                    i.then_inc(last, 1)

            def step(m, par, s):
                n = step_count(m, s)
                now = slice(s * B, (s + 1) * B)
                pr = rh_ps[par][:, 0, :, now]
                pe.wait_ge(st_hi, n)
                recur(pr, R, 0, state, 0)
                recur(pr, R, 1, state, 0)
                pe.wait_ge(st_low, n)
                recur(pr, R, 0, state, 1, r_done)
                for wpart in range(HPARTS):
                    for half in range(KC):
                        for k in range(KC):
                            i = mm(z_ps[par][:, :, half, now], whp[:, wpart, Z, k, half * P:(half + 1) * P],
                                   state[:, k], False, wpart == HPARTS - 1)
                i.then_inc(z_done, 1)

            def step_end(m, par, s):
                n = step_count(m, s)
                ph = rh_ps[par][:, 1, :, s * B:(s + 1) * B]
                pe.wait_ge(rh_hi, n)
                recur(ph, H, 0, rhp, 0)
                recur(ph, H, 1, rhp, 0)
                pe.wait_ge(rh_low, n)
                recur(ph, H, 0, rhp, 1, h_done)

            def between_z_h(m, par, s, has_y, has_l23, has_l0):
                m1, m2 = later(m, 1), later(m, 2)
                if has_l0:
                    if s == 0:
                        scores(m2, par)
                    if s == 3:
                        up_chunks(A1, sw1, par, (2,), a1_done, False)
                    if s == 6:
                        up_chunks(A3, sw3, par, (3,), a3_done, True)
                    if s == 7:
                        up_chunks(E47, rw1, par, (4,), ex47_done, False)
                    if s == 8:
                        up_chunks(E47, rw1, par, (5,), ex47_done, False)
                    if s == 9:
                        pe.wait_ge(sa_done, count(m2, 1))
                        up_chunks(A1, rw1, par, (0,), ex03_done, False)
                    if s == 10:
                        up_chunks(A1, rw1, par, (1,), ex03_done, False)
                    if s == 11:
                        spread_gates(m2, E47, (4, 5), cb47_done, False)
                    if s == 12:
                        spread_gates(m2, A3, (2, 3), cb03_done, True)
                    if s == 13:
                        l0_out(0, "s", (2, 3))
                    if s == 14:
                        l0_out(1, "s", (2, 3))
                    if s == 15:
                        pe.wait_ge(ge03_done, count(m2, 1))
                        l0_out(0, "r", (0, 1))
                if has_l23:
                    if s == 1:
                        low_in_rank(0, x2, u_done)
                    if s == 2:
                        mid_low(m1)
                    if s == 4:
                        low_in_rank(1, g2, v_done)
                    if s == 5:
                        up_low(m1)

            def between_steps(m, par, s, has_y, has_l23, has_l0):
                m1, m2 = later(m, 1), later(m, 2)
                q = 1 - par
                if has_l23:
                    if s == 0:
                        mid_base(m1)
                    if s == 3:
                        up_base(m1)
                    if s == 6:
                        pe.wait_ge(x3_done, count(m1, 1))
                        project(q, R, 0)
                        project(q, R, 1)
                    if s == 7:
                        project(q, Z, 0)
                        project(q, Z, 1)
                    if s == 9:
                        project(q, H, 0)
                        project(q, H, 1)
                if has_y and s == 1:
                    y_out(later(m, -1), q)
                if has_l0:
                    if s == 2:
                        up_chunks(A1, sw1, par, (0, 1), a1_done, False)
                    if s == 4:
                        up_chunks(A1, sw1, par, (3,), a1_done, True)
                        up_chunks(A3, sw3, par, (0,), a3_done, False)
                    if s == 5:
                        up_chunks(A3, sw3, par, (1, 2), a3_done, False)
                    if s == 8:
                        up_chunks(E47, rw1, par, (6, 7), ex47_done, True)
                    if s == 10:
                        up_chunks(A1, rw1, par, (2, 3), ex03_done, True)
                    if s == 11:
                        spread_gates(m2, E47, (6, 7), cb47_done, True)
                        pe.wait_ge(gs_done, count(m2, 1))
                        spread_gates(m2, A3, (0, 1), cb03_done, False)
                    if s == 12:
                        l0_out(0, "s", (0, 1), start=True)
                        l0_out(1, "s", (0, 1))
                    if s == 13:
                        pe.wait_ge(ge47_done, count(m2, 1))
                        l0_out(0, "r", (4, 5, 6, 7))
                    if s == 14:
                        l0_out(1, "r", (4, 5, 6, 7))
                    if s == 15:
                        l0_out(0, "r", (2, 3))
                        l0_out(1, "r", (0, 1, 2, 3), done=l0_done)

            def body(m, par, has_y, has_l23, has_l0):
                for s in range(STEPS):
                    step(m, par, s)
                    between_z_h(m, par, s, has_y, has_l23, has_l0)
                    step_end(m, par, s)
                    between_steps(m, par, s, has_y, has_l23, has_l0)

            pe.wait_ge(cond_in, 32)
            pe.wait_ge(l0_in, 32)
            for k in range(KC):
                i = mm(A1[:, 0:EXPERTS], cond_tok[:, k], rtw[:, k], k == 0, k == KC - 1)
            i.then_inc(setup_pe, 1)
            pe.wait_ge(l1_in, 32)
            for half in range(KC):
                for k in range(KC):
                    i = mm(A3[:, half * B:(half + 1) * B], l1w1[:, k, half * P:(half + 1) * P], condT[:, k],
                           k == 0, k == KC - 1)
            i.then_inc(setup_pe, 1)
            pe.wait_ge(ident_in, 16)
            pe.wait_ge(ready_dve, 1)
            for k in range(KC):
                i = mm(E47[:, k * B:(k + 1) * B], cn[:, k * P:(k + 1) * P], ident[0:B, 0:B], True, True)
            i.then_inc(setup_pe, 1)
            pe.wait_ge(l1w2_in, 16)
            pe.wait_ge(ready_dve, 2)
            for half in range(KC):
                for k in range(KC):
                    i = mm(gate_rh[1][:, half * B:(half + 1) * B], l1w2[:, k, half * P:(half + 1) * P], l1h[:, k],
                           k == 0, k == KC - 1)
            i.then_inc(setup_pe, 1)
            pe.wait_ge(ad_in, 32)
            pe.wait_ge(ready_dve, 3)
            for half in range(KC):
                for k in range(KC):
                    i = mm(E5[:, half * B:(half + 1) * B], aw1[:, k, half * P:(half + 1) * P], cT[:, k],
                           k == 0, k == KC - 1)
            i.then_inc(setup_pe, 1)

            def l0_whole_a(m, par):
                scores(m, par)
                pe.wait_ge(l0w_in, 32)
                up_chunks(A1, sw1, par, range(4), a1_done, True)
                up_chunks(A3, sw3, par, range(4), a3_done, True)
                pe.wait_ge(l0r_in, 48)
                pe.wait_ge(score_in, count(m, 1))
                up_chunks(E47, rw1, par, range(4, 8), ex47_done, True)
                pe.wait_ge(sa_done, count(m, 1))
                up_chunks(A1, rw1, par, range(0, 4), ex03_done, True)

            def l0_whole_b(m, par):
                pe.wait_ge(pe47_done, count(m, 1))
                spread_gates(m, E47, (4, 5, 6, 7), cb47_done, True)
                pe.wait_ge(gs_done, count(m, 1))
                spread_gates(m, A3, (0, 1, 2, 3), cb03_done, True)
                l0_out(0, "s", (0, 1, 2, 3), start=True)
                l0_out(1, "s", (0, 1, 2, 3))
                pe.wait_ge(ge47_done, count(m, 1))
                l0_out(0, "r", (4, 5, 6, 7))
                l0_out(1, "r", (4, 5, 6, 7))
                pe.wait_ge(ge03_done, count(m, 1))
                l0_out(0, "r", (0, 1, 2, 3))
                l0_out(1, "r", (0, 1, 2, 3), done=l0_done)

            l0_whole_a((0, 0), 0)
            pe.wait_ge(peaks_dve, 5)
            mm(gate_rh[0][0:4, 0:P], peak[:], ident[:], True, True).then_inc(peaks_pe, 1)
            pe.wait_ge(peaks_dve, 7)
            mm(gate_z[0][:, 0:4], ones4[:], peakd[:], True, True).then_inc(peaks_pe, 1)
            pe.wait_ge(setup_act, 2)
            l0_whole_b((0, 0), 0)
            pe.wait_ge(scales_done, 1)
            for c in range(ADAPT // 512):
                if c % 4 == 0:
                    pe.wait_ge(ad2_in[LOW_ORDER[c // 4]], 16)
                if c >= 3:
                    pe.wait_ge(wrow_dve, c - 2)
                at = LOW_ORDER[c // 4] * RANK * D + c % 4 * 512
                for k in range(KC):
                    i = mm(spare[c % 3][0:B, :], ah[:, k], aw2[:, k, at:at + 512], k == 0, k == KC - 1)
                i.then_inc(adapt_pe, 1)
            l0_whole_a((0, 1), 1)
            pe.wait_ge(ready_dve, 4)
            for i_, src in enumerate((2, 1)):
                for k in range(KC):
                    i = mm(gate_rh[0][:, (i_ * KC + k) * BR:(i_ * KC + k + 1) * BR], low[:, src, k * P:(k + 1) * P],
                           ident[0:BR, 0:BR], True, True)
            i.then_inc(lowT_pe, 1)
            m0 = (0, 0)
            pe.wait_ge(l2_in, 32)
            mid_base(m0)
            pe.wait_ge(ready_dve, 5)
            low_in_rank(0, x2, u_done)
            mid_low(m0)
            up_base(m0)
            low_in_rank(1, g2, v_done)
            up_low(m0)
            pe.wait_ge(x3_done, 1)
            pe.wait_ge(wx_scaled, 3)
            pe.wait_ge(scales_done, 2 + 3 * XPARTS)
            for g in (R, Z, H):
                for half in range(KC):
                    project(0, g, half)
            l0_whole_b((0, 1), 1)
            pe.wait_ge(split_w, 6)
            blocks(pe, body)
            y_out((0, BLOCKS - 1), 1)

        @block.scalar
        def _(act):
            def func(o, i, f, **kw):
                return act.activation(o, i, f, **kw)

            def tanh_a1(m):
                act.wait_ge(a1_done, count(m, 1))
                func(sig1[:], A1[:, :], ACT.Tanh, scale=0.5).then_inc(a1_sig, 1)

            def gelu_experts(m, group, p_, ready, done):
                act.wait_ge(ready, count(m, 1))
                func(pe_e[:, group], p_[:, :], ACT.Gelu).then_inc(done, 1)

            def gelu_mid(m):
                act.wait_ge(mid_done, count(m, 1))
                func(g2[:], mid_ps, ACT.Gelu).then_inc(g2_done, 1)

            def after(m, par, s, has_y, has_l23, has_l0):
                m1, m2 = later(m, 1), later(m, 2)
                q = 1 - par
                if has_l23:
                    if s == 2:
                        gelu_mid(m1)
                if has_l0:
                    if s == 5:
                        tanh_a1(m2)
                    if s == 9:
                        gelu_experts(m2, 1, E47, ex47_done, pe47_done)
                    if s == 11:
                        gelu_experts(m2, 0, A1, ex03_done, pe03_done)

            tanh_scale = [act.alloc_register(f"tanh_scale{g}") for g in range(3)]

            def body(m, par, has_y, has_l23, has_l0):
                for s in range(STEPS):
                    n = step_count(m, s)
                    now = slice(s * B, (s + 1) * B)
                    act.wait_ge(r_done, n)
                    func(rg[:], rh_ps[par][:, 0, :, now], ACT.Tanh, scale=tanh_scale[R]).then_inc(rg_done, 1)
                    act.wait_ge(zsum_done, n)
                    func(zg[:], zsum[:], ACT.Tanh, scale=tanh_scale[Z]).then_inc(zg_done, 1)
                    act.wait_ge(h_done, n)
                    func(ht[:], rh_ps[par][:, 1, :, now], ACT.Tanh, scale=tanh_scale[H]).then_inc(ht_done, 1)
                    after(m, par, s, has_y, has_l23, has_l0)

            act.wait_ge(setup_dve, 6)
            func(l1sig[:], l1pre[:], ACT.Tanh, scale=0.5).then_inc(setup_act, 1)
            act.wait_ge(setup_pe, 5)
            for half in range(KC):
                i = func(ah[:, half], E5[:, half * B:(half + 1) * B], ACT.Gelu, bias=lnab[:, 2, half:half + 1])
            i.then_inc(setup_act, 1)
            act.wait_ge(setup_dve, 8)
            func(l1sig[:], l1pre[:], ACT.Tanh, scale=0.5).then_inc(setup_act, 1)
            m0, m1 = (0, 0), (0, 1)
            tanh_a1(m0)
            gelu_experts(m0, 1, E47, ex47_done, pe47_done)
            gelu_experts(m0, 0, A1, ex03_done, pe03_done)
            tanh_a1(m1)
            gelu_experts(m1, 1, E47, ex47_done, pe47_done)
            gelu_experts(m1, 0, A1, ex03_done, pe03_done)
            gelu_mid(m0)
            act.wait_ge(scales_done, 1)
            for g in (Z, R, H):
                act.reg_load(tanh_scale[g], unscale[0:1, g:g + 1].bitcast(U32))
            blocks(act, body)

        @block.vector
        def _(dve):
            def add_router_bias(m):
                dve.wait_ge(scores_done, count(m, 1))
                dve.scalar_tensor_tensor(score[:], score_ps, -1.0, tbias[:], ALU.mult, ALU.subtract)\
                   .then_inc(score_in, 1)

            def gate_op(m, k):
                if k == 0:
                    dve.wait_ge(score_exp, count(m, 1))
                    i = dve.tensor_scalar(exp1[:], expn[:], 1.0, None, ALU.add)
                else:
                    dve.wait_ge(gating, count(m, GATE_OPS, k - GATE_OPS))
                if k in (3, 4):
                    dve.memset(holder[:], 0.0)
                if k == 1:
                    i = dve.reciprocal(sg[:], exp1[:])
                if k == 2:
                    i = dve.tensor_tensor(sel[:], sg[:], rbias[:], ALU.add)
                if k == 3:
                    i = dve.max(top8[:], sel[:])
                if k == 4:
                    i = dve.max_index(idx[:], top8[:], sel[:])
                if k == 5:
                    i = dve.tensor_copy(idxf[:], idx[:, 0:2])
                if k == 6:
                    i = dve.tensor_scalar(first[:], iota[:], idxf[:, 0:1], None, ALU.is_equal)
                if k == 7:
                    i = dve.scalar_tensor_tensor(chosen[:], iota[:], idxf[:, 1:2], first[:], ALU.is_equal, ALU.add)
                if k == 8:
                    i = dve.scalar_tensor_tensor(ssel[:], sg[:], 1.0, chosen[:], ALU.mult, ALU.mult,
                                                 accum_out=den[:, 0:1])
                if k == 9:
                    dve.tensor_scalar(den[:, 1:2], den[:, 0:1], EPS_GATE, 2.0, ALU.is_gt, ALU.mult)
                    i = dve.tensor_scalar(den[:, 2:3], den[:, 0:1], EPS_GATE, None, ALU.add)
                if k == 10:
                    dve.tensor_scalar(den[:, 3:4], den[:, 1:2], -0.5, 1.0, ALU.mult, ALU.add)
                    i = dve.reciprocal(den[:, 2:3], den[:, 2:3])
                if k == 11:
                    i = dve.tensor_scalar(scaled[:], ssel[:], den[:, 2:3], den[:, 1:2], ALU.mult, ALU.mult)
                if k == 12:
                    i = dve.scalar_tensor_tensor(comb[:], chosen[:], den[:, 3:4], scaled[:], ALU.mult, ALU.add)
                i.then_inc(gating, 1)

            def silu_a1(m):
                dve.wait_ge(a1_sig, count(m, 1))
                dve.scalar_tensor_tensor(sa[:], sig1[:], 1.0, A1[:, :], ALU.add, ALU.mult).then_inc(sa_done, 1)

            def times_a3(m):
                dve.wait_ge(a3_done, count(m, 1))
                dve.wait_ge(sa_done, count(m, 1))
                dve.tensor_tensor(gs[:], sa[:], A3[:, :], ALU.mult).then_inc(gs_done, 1)

            def times_gate(m, group, p_, ready, mine, done):
                dve.wait_ge(ready, count(m, 1))
                dve.wait_ge(mine, count(m, 1))
                dve.tensor_tensor(ge[:, group], pe_e[:, group], p_[:, :], ALU.mult).then_inc(done, 1)

            def finish_l0(m, par):
                dve.wait_ge(l0_done, count(m, 1))
                dve.scalar_tensor_tensor(x1[:], l0_ps, 1.0 / 6.0, xt[:, par], ALU.mult, ALU.add).then_inc(x1_done, 1)

            def l1(m):
                dve.wait_ge(x1_done, count(m, 1))
                g = gate2[:].unsqueeze(2).to_broadcast([P, KC, STEPS, B])
                dve.tensor_tensor(x2[:].rearrange("p k (t b) -> p k t b", b=B),
                                  x1[:].rearrange("p k (t b) -> p k t b", b=B), g, ALU.mult).then_inc(x2_done, 1)

            def keep_own(m, dst, ready, done):
                dve.wait_ge(ready, count(m, 1))
                dve.tensor_tensor(dst[:], own[:], low_ps, ALU.mult).then_inc(done, 1)

            def finish_l2(m, par):
                dve.wait_ge(l2_done, count(m, 1))
                dve.scalar_tensor_tensor(x3[:, par], x2[:], 2.0, mid_ps, ALU.mult, ALU.add).then_inc(x3_done, 1)

            def y_add(m, par):
                dve.wait_ge(y_done, count(m, 1))
                if not (type(m[0]) is int and m[1] == 0):
                    dve.wait_ge(stored, count(m, 16, -16))
                for half in range(KC):
                    i = dve.scalar_tensor_tensor(osb[:, half], y_ps[:, half], bq[:, half:half + 1], x3[:, par, half],
                                                 ALU.add, ALU.add)
                i.then_inc(out_done, 1)

            def early(m, par, s, has_y, has_l23, has_l0):
                m1, m2 = later(m, 1), later(m, 2)
                q = 1 - par
                if has_l23:
                    if s == 0:
                        finish_l0(m1, q)
                    if s == 2:
                        keep_own(m1, um, u_done, um_done)
                    if s == 5:
                        keep_own(m1, vm, v_done, vm_done)
                    if s == 6:
                        finish_l2(m1, q)
                if has_y and s == 2:
                    y_add(later(m, -1), q)
                if has_l0:
                    if s == 1:
                        add_router_bias(m2)
                    if s == 4:
                        gate_op(m2, 0)
                    if s == 6:
                        silu_a1(m2)
                    if s == 5:
                        gate_op(m2, 2)
                    if s == 7:
                        gate_op(m2, 6)
                    if s == 8:
                        times_a3(m2)
                    if s == 10:
                        gate_op(m2, 11)
                    if s == 12:
                        times_gate(m2, 1, E47, cb47_done, pe47_done, ge47_done)
                    if s == 14:
                        times_gate(m2, 0, A3, cb03_done, pe03_done, ge03_done)

            def late(m, par, s, has_y, has_l23, has_l0):
                m1, m2 = later(m, 1), later(m, 2)
                q = 1 - par
                if has_l23:
                    if s == 0:
                        l1(m1)
                if has_l0:
                    for at, k in ((4, 1), (5, 3), (6, 4), (6, 5), (7, 7), (8, 8), (9, 9), (9, 10), (10, 12)):
                        if s == at:
                            gate_op(m2, k)

            def body(m, par, has_y, has_l23, has_l0):
                for s in range(STEPS):
                    n = step_count(m, s)
                    bp, bs = before(par, s)
                    old = hist[:, bp, :, bs * B:(bs + 1) * B]
                    new = hist[:, par, :, s * B:(s + 1) * B]
                    early(m, par, s, has_y, has_l23, has_l0)
                    dve.wait_ge(rg_done, n)
                    dve.scalar_tensor_tensor(rhp[:, :, 0], rg[:], 1.0, old, ALU.add, ALU.mult).then_inc(rh_hi, 1)
                    dve.scalar_tensor_tensor(rh[:], rg[:], 1.0, old, ALU.add, ALU.mult).then_inc(rh_all, 1)
                    z_now = z_ps[par][:, :, :, s * B:(s + 1) * B]
                    dve.wait_ge(z_done, n)
                    dve.tensor_reduce(zsum[:], z_now.rearrange("p a k c -> p k c a"), AX_X, ALU.add).then_inc(zsum_done, 1)
                    dve.wait_ge(rh_all, n)
                    dve.tensor_tensor(rhp[:, :, 1], rh[:], rhp[:, :, 0], ALU.subtract).then_inc(rh_low, 1)
                    late(m, par, s, has_y, has_l23, has_l0)
                    dve.wait_ge(zg_done, n)
                    dve.tensor_scalar(zm[:], zg[:], -1.0, sscale[:], ALU.add, ALU.mult).then_inc(zm_done, 1)
                    dve.wait_ge(zm_done, n)
                    dve.scalar_tensor_tensor(zh[:], zg[:], 1.0, old, ALU.add, ALU.mult)
                    dve.wait_ge(ht_done, n)
                    dve.tensor_tensor(fresh[:], zm[:], ht[:], ALU.mult).then_inc(fresh_done, 1)
                    dve.wait_ge(fresh_done, n)
                    dve.scalar_tensor_tensor(state[:, :, 0], zh[:], 0.5, fresh[:], ALU.mult, ALU.subtract)\
                       .then_inc(st_hi, 1)
                    dve.scalar_tensor_tensor(new, zh[:], 0.5, fresh[:], ALU.mult, ALU.subtract).then_inc(st_all, 1)
                    dve.wait_ge(st_all, n + 1)
                    dve.tensor_tensor(state[:, :, 1], new, state[:, :, 0], ALU.subtract).then_inc(st_low, 1)

            c_ = [0]

            def link(i):
                c_[0] += 1
                i.then_inc(setup_dve, 1)
                dve.wait_ge(setup_dve, c_[0])

            dve.wait_ge(cond_in, 32)
            link(dve.bn_stats(stats[:], cond[:]))
            link(dve.bn_aggr(meanvar[:], stats[:]))
            dve.memset(lnv[:, 1:2], -0.5)
            link(dve.tensor_scalar(lnv[:, 0:1], meanvar[:, 1:2], EPS_LN, None, ALU.add))
            dve.wait_ge(setup_pool, 1)
            dve.tensor_scalar(cn[:], cond[:], meanvar[:, 0:1], lnv[:, 2:3], ALU.subtract, ALU.mult).then_inc(ready_dve, 1)
            dve.wait_ge(setup_pe, 1)
            link(dve.tensor_copy(tbias[:], A1[:, 0:EXPERTS]))
            dve.wait_ge(setup_pe, 2)
            dve.wait_ge(l1_in, 32)
            for half in range(KC):
                link(dve.tensor_scalar(l1pre[:, half], A3[:, half * B:(half + 1) * B], l1b[:, 0, half:half + 1], None,
                                       ALU.add))
            dve.wait_ge(setup_act, 1)
            dve.scalar_tensor_tensor(l1h[:], l1sig[:], 1.0, l1pre[:], ALU.add, ALU.mult).then_inc(ready_dve, 1)
            dve.wait_ge(setup_pe, 3)
            dve.wait_ge(ad_in, 32)
            for k in range(KC):
                i = dve.tensor_scalar(cT[:, k], E47[:, k * B:(k + 1) * B], lnab[:, 0, k:k + 1], lnab[:, 1, k:k + 1],
                                      ALU.mult, ALU.add)
            i.then_inc(ready_dve, 1)
            dve.wait_ge(setup_pe, 4)
            for half in range(KC):
                link(dve.tensor_scalar(l1pre[:, half], gate_rh[1][:, half * B:(half + 1) * B], 0.5, l1b[:, 1, half:half + 1],
                                       ALU.mult, ALU.add))
            dve.wait_ge(setup_act, 3)
            link(dve.tensor_scalar(gate2[:], l1sig[:], 0.5, 2.5, ALU.mult, ALU.add))
            dve.memset(ones_row[:], 1.0)

            def find_scales():
                dve.memset(ones4[:], 1.0)
                dve.wait_ge(rec_in, 48)
                for g in range(3):
                    dve.tensor_reduce(peak[:, g:g + 1], wh[:, g], AX_XY, ALU.max, apply_absolute_value=True)\
                       .then_inc(peaks_dve, 1)
                dve.tensor_reduce(peak[:, 3:4], condT, AX_XY, ALU.max, apply_absolute_value=True).then_inc(peaks_dve, 1)
                dve.wait_ge(peaks_dve, 4)
                dve.tensor_scalar(peak[:, 3:4], peak[:, 3:4], 1.0, None, ALU.max).then_inc(peaks_dve, 1)
                dve.wait_ge(peaks_pe, 1)
                dve.tensor_reduce(peak4[:], gate_rh[0][0:4, 0:P], AX_X, ALU.max).then_inc(peaks_dve, 1)
                dve.wait_ge(peaks_dve, 6)
                dve.tensor_scalar(peakd[:], ident[0:4, 0:4], peak4[:], None, ALU.mult).then_inc(peaks_dve, 1)
                dve.wait_ge(peaks_pe, 2)
                dve.tensor_scalar(inv[:], gate_z[0][:, 0:4], LEAST_PEAK, None, ALU.max).then_inc(peaks_dve, 1)
                dve.wait_ge(peaks_dve, 8)
                dve.tensor_scalar(power[:].bitcast(U32), inv[:].bitcast(U32), EXPONENT_BITS, None, ALU.bitwise_and)\
                   .then_inc(peaks_dve, 1)
                dve.wait_ge(peaks_dve, 9)
                dve.reciprocal(inv[:], power[:]).then_inc(peaks_dve, 1)
                dve.wait_ge(peaks_dve, 10)
                dve.tensor_scalar(wscale[:], inv[:, 0:3], 2.0 ** W_TOP, None, ALU.mult)
                dve.tensor_scalar(sscale[:], inv[:, 3:4], 2.0 ** S_TOP, None, ALU.mult)
                dve.tensor_scalar(qscale[:], power[:, 3:4], 0.5 * 2.0 ** -S_TOP, None, ALU.mult)
                for g, times, half in ((Z, 2.0, 0.5), (R, 2.0, 0.5), (H, 4.0, 1.0)):
                    top = 2.0 ** (W_TOP + S_TOP) * times
                    dve.tensor_scalar(xscale[:, g:g + 1], inv[:, g:g + 1], inv[:, 3:4], top, ALU.mult, ALU.mult)
                    i = dve.tensor_scalar(unscale[:, g:g + 1], power[:, g:g + 1], power[:, 3:4], half / top,
                                          ALU.mult, ALU.mult)
                i.then_inc(scales_done, 1)
                dve.wait_ge(bias_in, 16 * 2)
                dve.tensor_tensor(bx[:], bx[:], bh[:], ALU.add).then_inc(peaks_dve, 1)
                dve.wait_ge(peaks_dve, 11)
                for g in range(3):
                    i = dve.tensor_scalar(bx[:, g], bx[:, g], xscale[0:XPARTS, g:g + 1], None, ALU.mult)
                i.then_inc(scales_done, 1)
                rows = ident[0:XPARTS]
                for part in range(XPARTS):
                    dve.wait_ge(scales_done, 2 + 3 * part)
                    dve.tensor_copy(bpart[:, part % 2], bx[:]).then_inc(scales_done, 1)
                    dve.wait_ge(scales_done, 3 + 3 * part)
                    dve.tensor_tensor(bx[:], bx[:], bpart[:, part % 2], ALU.subtract).then_inc(scales_done, 1)
                    if part == 0:
                        i = dve.tensor_scalar(brow[:], bpart[:, 0], rows[:, 0:1], None, ALU.mult)
                    else:
                        i = dve.scalar_tensor_tensor(brow[:], bpart[:, part % 2], rows[:, part:part + 1], brow[:],
                                                     ALU.mult, ALU.add)
                    i.then_inc(scales_done, 1)

            def gates_whole(m):
                for k in range(GATE_OPS):
                    gate_op(m, k)

            def l0_whole_a(m):
                add_router_bias(m)
                gates_whole(m)
                silu_a1(m)
                times_a3(m)

            def l0_whole_b(m):
                times_gate(m, 1, E47, cb47_done, pe47_done, ge47_done)
                times_gate(m, 0, A3, cb03_done, pe03_done, ge03_done)

            m0, m1 = (0, 0), (0, 1)
            dve.wait_ge(const_in, 16 * 3)
            l0_whole_a(m0)
            find_scales()
            dve.tensor_scalar(sscale2[:], sscale[:], 2.0, None, ALU.mult).then_inc(peaks_dve, 1)
            dve.wait_ge(peaks_dve, 12)
            last = hist[:, 1, :, (STEPS - 1) * B:STEPS * B]
            dve.tensor_scalar(state[:, :, 0], condT, sscale2[:], None, ALU.mult).then_inc(st_hi, 1)
            dve.tensor_scalar(last, condT, sscale2[:], None, ALU.mult).then_inc(st_all, 1)
            dve.wait_ge(st_all, 1)
            dve.tensor_tensor(state[:, :, 1], last, state[:, :, 0], ALU.subtract).then_inc(st_low, 1)
            l0_whole_b(m0)
            finish_l0(m0, 0)
            l1(m0)
            for c in range(ADAPT // 512):
                dve.wait_ge(adapt_pe, c + 1)
                if c >= 8 and c % 4 == 0:
                    dve.wait_ge(low_in[LOW_ORDER[c // 4 - 2]], B * 16)
                dve.tensor_copy(wrow[:, c // 4 % 2, c % 4 * 512:(c % 4 + 1) * 512], spare[c % 3][0:B, :])\
                   .then_inc(wrow_dve, 1)
            l0_whole_a(m1)
            for i in LOW_ORDER:
                dve.wait_ge(low_in[i], B * 16)
            dve.wait_ge(abias_in, 16 * B)
            dve.tensor_tensor(low[:], low[:], abias[:], ALU.add).then_inc(ready_dve, 1)
            dve.wait_ge(lowT_pe, 1)
            dve.tensor_copy(a2b1[:], gate_rh[0][:, 0:2 * KC * BR].rearrange("p (i k c) -> p i k c", i=2, k=KC))\
               .then_inc(ready_dve, 1)
            keep_own(m0, um, u_done, um_done)
            keep_own(m0, vm, v_done, vm_done)
            finish_l2(m0, 0)
            l0_whole_b(m1)
            dve.wait_ge(bq_in, 16)
            blocks(dve, body)
            y_add((0, BLOCKS - 1), 1)


def kernel(**inputs):
    import concourse.bacc as _bacc
    from concourse.bass_utils import run_bass_kernel_spmd as _run

    f = {k: np.asarray(v) for k, v in inputs.items()}

    def rows(w):
        return np.ascontiguousarray(w.reshape(-1, P, w.shape[-1]).transpose(1, 0, 2))

    def vec(v):
        return v.reshape(KC, P).T

    g3 = ("z", "r", "h")
    L0, L1, L2, L3 = ("L0_cond_", "L1_cond_", "L2_cond_", "L3_cond_")
    w2 = f[L2 + "W2"].reshape(D, 4, D, RANK).transpose(0, 1, 3, 2).reshape(D, ADAPT)
    tok = np.arange(TOK)
    arrays = {
        "xT": rows(f["x"].transpose(2, 1, 0).reshape(D, T * B)),
        "cond_tok": rows(f["cond_1024"].T[:, tok % B]),
        "cond": f["cond_1024"],
        "sw1": rows(f[L0 + "sw1"].T), "sw3": rows(f[L0 + "sw3"].T), "sw2": rows(f[L0 + "sw2"].T),
        "rw1": rows(f[L0 + "rw1"].reshape(EXPERTS * HR, D).T),
        "rw2": rows(f[L0 + "rw2"].transpose(0, 2, 1).reshape(EXPERTS * HR, D)),
        "rw": rows(f[L0 + "router_w"].T), "rtw": rows(f[L0 + "router_t_w"].T), "rbias": f[L0 + "router_bias"],
        "l1w1": rows(f[L1 + "W1"].T), "l1w2": rows(f[L1 + "W2"].T),
        "l1b": np.stack([vec(f[L1 + "b1"]), vec(f[L1 + "b2"])], 1),
        "down": rows(f[L2 + "base_down"]), "up": rows(f[L2 + "base_up"].T),
        "aw1": rows(f[L2 + "W1"]), "aw2": rows(w2),
        "lnab": np.stack([vec(f[L2 + n]) for n in ("ln_gamma", "ln_beta", "bias1")], 1),
        "abias": f[L2 + "bias2"].reshape(4, D, RANK).transpose(2, 0, 1),
        "wx": np.stack([rows(f[L3 + "Wx" + g].T) for g in g3]),
        "wh": np.stack([rows(f[L3 + "Wh" + g].T) for g in g3]),
        "wq": rows(f[L3 + "Whq"].T),
        "bx": np.stack([f[L3 + "bx" + g] for g in g3]),
        "bh": np.stack([f[L3 + "bh" + g] for g in g3]),
        "bq": vec(f[L3 + "bhq"]),
        "ident": np.eye(P, dtype=np.float32),
        "iota": np.tile(np.arange(EXPERTS, dtype=np.float32), (P, 1)),
        "own": (np.arange(BR)[:, None] // RANK == tok[None] % B).astype(np.float32),
    }
    nc = _bacc.Bacc("TRN2", target_bir_lowering=False, num_devices=1)
    feeds, handles = {}, {}
    for name, v in arrays.items():
        v = np.ascontiguousarray(v)
        feeds[f"in_{name}"] = v
        handles[name] = nc.dram_tensor(f"in_{name}", v.shape, mybir.dt.from_np(v.dtype), kind="ExternalInput").ap()
    out = nc.dram_tensor("out_0", (P, KC, T * B), F32, kind="ExternalOutput").ap()
    build(nc, handles, out)
    r = _run(nc, [feeds], core_ids=[0])
    got = r.results[0]["out_0"]
    return np.ascontiguousarray(got.reshape(P, KC, T, B).transpose(3, 2, 1, 0).reshape(B, T, D))
```
